# Optimizing a Trainium2 kernel written in Bass

```python
import numpy as np
import jax
import jax.numpy as jnp

def _softmax(x, axis=-1):
    return jax.nn.softmax(x, axis=axis)

def _gelu(x):
    return jax.nn.gelu(x, approximate=True)

def _silu(x):
    return jax.nn.silu(x)

def _sigmoid(x):
    return jax.nn.sigmoid(x)

def _layernorm(x, axis=-1, eps=1e-05):
    m = jnp.mean(x, axis=axis, keepdims=True)
    v = jnp.var(x, axis=axis, keepdims=True)
    return (x - m) / jnp.sqrt(v + eps)

def _scatter_add(tgt, idx, src, axis=0):
    return tgt.at[idx].add(src)

def _segment_sum(src, seg, n):
    return jax.ops.segment_sum(src, seg, n)
kernel_name = 'mk_rec_standalone_d1_rec_r8_1de338'

def setup_inputs(seed: int=0):
    np.random.seed(seed)
    _w = jnp.asarray

    def _rec_inputs():
        import jax
        import jax.numpy as jnp
        _rk = jax.random.key(seed)
        r_hist_items = -0.000161372 + 0.999968 * jax.random.normal(jax.random.fold_in(_rk, 1), (2048, 200, 128), jnp.float32)
        r_hist_mask = jax.random.bernoulli(jax.random.fold_in(_rk, 2), 0.5013, (2048, 200))
        r_hist_age_hours = jax.random.uniform(jax.random.fold_in(_rk, 3), (2048, 200), jnp.float32, 0.0, 168)
        r_hist_popularity = jax.random.uniform(jax.random.fold_in(_rk, 4), (2048, 200), jnp.float32, 0.0, 0.999999)
        return (r_hist_items, r_hist_mask, r_hist_age_hours, r_hist_popularity)
    r_hist_items, r_hist_mask, r_hist_age_hours, r_hist_popularity = _rec_inputs()

    def _L0_rec_setup():
        import jax, jax.numpy as jnp
        import numpy as np
        B, T, D = (512, 200, 128)
        K_SHORT = 5
        key = jax.random.key(seed)
        ks = jax.random.split(key, 8)
        hist_items = jax.random.normal(ks[0], (B, T, D), dtype=jnp.float32)
        hist_mask = jax.random.randint(ks[1], (B, T), 0, 2).astype(bool)
        hist_mask = hist_mask.at[:, 0].set(True)
        hist_age_hours = jax.random.uniform(ks[2], (B, T), dtype=jnp.float32) * 168.0
        hist_popularity = jax.random.uniform(ks[3], (B, T), dtype=jnp.float32)
        s = 1.0 / float(np.sqrt(D))
        Wq = jax.random.normal(ks[4], (D, D), dtype=jnp.float32) * s
        Wk = jax.random.normal(ks[5], (D, D), dtype=jnp.float32) * s
        Wv = jax.random.normal(ks[6], (D, D), dtype=jnp.float32) * s
        gate_w = jax.random.normal(ks[7], (1, 2), dtype=jnp.float32) * 0.5
        gate_b = jnp.zeros((1,), dtype=jnp.float32)
        ln_gamma = jnp.ones((D,), dtype=jnp.float32)
        ln_beta = jnp.zeros((D,), dtype=jnp.float32)
        decay_alpha = jnp.asarray(0.05, dtype=jnp.float32)
        return {'hist_items': hist_items, 'hist_mask': hist_mask, 'hist_age_hours': hist_age_hours, 'hist_popularity': hist_popularity, 'Wq': Wq, 'Wk': Wk, 'Wv': Wv, 'gate_w': gate_w, 'gate_b': gate_b, 'ln_gamma': ln_gamma, 'ln_beta': ln_beta, 'decay_alpha': decay_alpha}
    _L0_rec_all = _L0_rec_setup()
    _L0_rec_in = {k: v for k, v in _L0_rec_all.items() if k in ('Wq', 'Wk', 'Wv', 'gate_w', 'gate_b', 'ln_gamma', 'ln_beta', 'decay_alpha')}
    del _L0_rec_all
    return {'r_hist_items': r_hist_items, 'r_hist_mask': r_hist_mask, 'r_hist_age_hours': r_hist_age_hours, 'r_hist_popularity': r_hist_popularity, 'L0_rec_Wq': _L0_rec_in['Wq'], 'L0_rec_Wk': _L0_rec_in['Wk'], 'L0_rec_Wv': _L0_rec_in['Wv'], 'L0_rec_gate_w': _L0_rec_in['gate_w'], 'L0_rec_gate_b': _L0_rec_in['gate_b'], 'L0_rec_ln_gamma': _L0_rec_in['ln_gamma'], 'L0_rec_ln_beta': _L0_rec_in['ln_beta'], 'L0_rec_decay_alpha': _L0_rec_in['decay_alpha']}

def reference(r_hist_items, r_hist_mask, r_hist_age_hours, r_hist_popularity, L0_rec_Wq, L0_rec_Wk, L0_rec_Wv, L0_rec_gate_w, L0_rec_gate_b, L0_rec_ln_gamma, L0_rec_ln_beta, L0_rec_decay_alpha):
    import jax
    import jax.numpy as jnp

    def _L0_rec_ref(hist_items, hist_mask, hist_age_hours, hist_popularity, Wq, Wk, Wv, gate_w, gate_b, ln_gamma, ln_beta, decay_alpha):
        import jax, jax.numpy as jnp
        import numpy as np
        B, T, D = (512, 200, 128)
        K_SHORT = 5
        dt = hist_items.dtype
        maskf = hist_mask.astype(dt)
        alpha = jax.nn.softplus(decay_alpha) + 1e-06
        decay = jnp.exp(-alpha * hist_age_hours) * maskf
        mean_hist = (hist_items * maskf[..., None]).sum(1) / (maskf.sum(1, keepdims=True) + 1e-06)
        q = mean_hist @ Wq.T
        k = jnp.einsum('btd,ed->bte', hist_items, Wk)
        v = jnp.einsum('btd,ed->bte', hist_items, Wv)
        scale = 1.0 / float(np.sqrt(hist_items.shape[-1]))
        scores = jnp.einsum('bd,btd->bt', q, k) * scale + jnp.log(decay + 1e-12)
        scores = jnp.where(hist_mask, scores, -jnp.inf)
        attn = jax.nn.softmax(scores, axis=-1)
        long_term = jnp.einsum('bt,btd->bd', attn, v)
        cnt = jnp.maximum(hist_mask.sum(1), 1)
        K = min(K_SHORT, hist_items.shape[1])
        ar = jnp.arange(hist_items.shape[1])[None, :]
        lastk = (ar >= cnt[:, None] - K) & (ar < cnt[:, None])
        lk = lastk.astype(dt)
        denom = jnp.maximum(lk.sum(1, keepdims=True), 1.0)
        short_term = (hist_items * lk[..., None]).sum(1) / denom
        mean_pop = (hist_popularity * lk).sum(1) / denom[:, 0]
        mean_rec = (hist_age_hours * lk).sum(1) / denom[:, 0]
        ctx = jnp.stack([mean_pop, mean_rec], axis=-1)
        g = jax.nn.sigmoid(ctx @ gate_w.T + gate_b)
        user = g * short_term + (1.0 - g) * long_term
        mu = user.mean(-1, keepdims=True)
        var = user.var(-1, keepdims=True)
        return (user - mu) / jnp.sqrt(var + 1e-05) * ln_gamma + ln_beta
    y = _L0_rec_ref(r_hist_items, r_hist_mask, r_hist_age_hours, r_hist_popularity, L0_rec_Wq, L0_rec_Wk, L0_rec_Wv, L0_rec_gate_w, L0_rec_gate_b, L0_rec_ln_gamma, L0_rec_ln_beta, L0_rec_decay_alpha)
    return y

_drawn_inputs = setup_inputs


def setup_inputs(seed=0):
    import zlib

    import numpy as np

    out = dict(_drawn_inputs(seed))
    spreads = {'L0_rec_ln_gamma': (1.0, 0.2), 'L0_rec_ln_beta': (0.0, 0.1)}
    factors = {'r_hist_popularity': 64.0, 'L0_rec_gate_w': 8.0}
    for name, (base, spread) in spreads.items():
        noise = np.random.default_rng([zlib.crc32(name.encode()), seed]).standard_normal(out[name].shape)
        drawn = base * np.exp(spread * noise) if base else spread * noise
        out[name] = jnp.asarray(drawn.astype(out[name].dtype))
    for name, factor in factors.items():
        out[name] = (out[name] * factor).astype(out[name].dtype)
    return out
```

```python
from contextlib import ExitStack

import concourse.bass as bass
from concourse import mybir

F32 = mybir.dt.float32
BF16 = mybir.dt.bfloat16
I32 = mybir.dt.int32
U8 = mybir.dt.uint8
ALU = mybir.AluOpType
ACT = mybir.ActivationFunctionType
AX_X = mybir.AxisListType.X

P = 128
USERS_PER_CHUNK = 16
CHUNKS = 4
STRIP = P // CHUNKS
GROUP = USERS_PER_CHUNK * CHUNKS
BLOCKS = P // USERS_PER_CHUNK
WINDOW = 5
X_SLOTS = 3
UNROLL = 6
TILE_RING = UNROLL // 2
FIRST_LOOP, LOOPS = 6, 4
MASKED = -1.0e30
PIECES = 5
SV = 13

SV_HALF = (SV + 1) // 2


class Step:

    def __init__(self, const, it=None, stride=UNROLL):
        self.const, self.it, self.stride = const, it, stride

    def __add__(self, n):
        return Step(self.const + n, self.it, self.stride)

    def __sub__(self, n):
        return self + -n

    def per(self, n):
        return Step(self.const // n, self.it, self.stride // n)

    def times(self, factor, plus=0):
        if self.it is None:
            return factor * self.const + plus
        return self.it * (factor * self.stride) + (factor * self.const + plus)

    def inside(self, first, end):
        return self.it is not None or first <= self.const < end


def wait(eng, sem, value):
    if not isinstance(value, int) or value > 0:
        eng.wait_ge(sem, value)


def hold(eng, sem, value, held):
    wait(eng, sem, value)
    eng.sem_inc(held, 1)


def run_steps(eng, step, first, last):
    for i in range(first, FIRST_LOOP):
        step(Step(i))
    with eng.Fori(0, LOOPS) as it:
        for u in range(UNROLL):
            step(Step(FIRST_LOOP + u, it))
    for i in range(FIRST_LOOP + UNROLL * LOOPS, last + 1):
        step(Step(i))


def build(nc, items, mask, age, popularity, Wq, Wk, Wv, gate_w, gate_b, ln_gamma, ln_beta, decay_alpha, out):
    USERS, T, D = items.shape
    J = T // BLOCKS
    JP = J // PIECES
    GROUPS = USERS // GROUP
    TILES = USERS // P
    SP_ = J - SV
    SCALE = 1.0 / float(D) ** 0.5
    assert D == P and GROUPS >= FIRST_LOOP + UNROLL * LOOPS

    items_g = items.rearrange("(g c b) (t j) d -> g (b t) c (j d)", c=CHUNKS, b=USERS_PER_CHUNK, t=BLOCKS)
    rows = items.rearrange("u t d -> (u t) d")
    age_t = age.rearrange("(k p) t -> k p t", p=P)
    pop_t = popularity.rearrange("(k p) t -> k p t", p=P)
    mask_t = mask.rearrange("(k p) t -> k p t", p=P)
    out_t = out.rearrange("(k p) d -> k p d", p=P)

    ctx = ExitStack()
    with ctx:
        def sb(name, shape, dt=F32):
            return ctx.enter_context(nc.sbuf_tensor(name, shape, dt))

        def ps(name):
            return ctx.enter_context(nc.psum_tensor(name, [P, 512], F32))

        def sem(name):
            return ctx.enter_context(nc.semaphore(name))

        x = [sb(f"x{s}", [P, CHUNKS, J, D]) for s in range(X_SLOTS)]
        products = [sb(f"products{s}", [P, SP_, D]) for s in range(2)]
        mask_w = [sb(f"mask_w{s}", [P, CHUNKS, J, USERS_PER_CHUNK]) for s in range(2)]
        attn_w = sb("attn_w", [P, CHUNKS, J, USERS_PER_CHUNK])
        query_sb = sb("query_sb", [P, CHUNKS, D])
        unused_v = sb("unused_v", [P, SV, D], BF16)
        logs_p = [sb(f"logs_p{s}", [P, CHUNKS, J + 1]) for s in range(UNROLL)]
        raw = [sb(f"raw{s}", [P, CHUNKS, J]) for s in range(2)]
        logits = sb("logits", [P, CHUNKS, J])
        exps = sb("exps", [P, CHUNKS, J])
        maxes = sb("maxes", [P, CHUNKS])
        gmax = sb("gmax", [CHUNKS, USERS_PER_CHUNK])
        gmax_wide = sb("gmax_wide", [CHUNKS, USERS_PER_CHUNK, BLOCKS])
        exp_sums = sb("exp_sums", [P, CHUNKS])
        sums_sb = sb("sums_sb", [P, D])
        mean_t = sb("mean_t", [P, GROUP, BLOCKS])
        inv_den = sb("inv_den", [P, 1])
        attended = sb("attended", [P, D])
        attended_t = sb("attended_t", [P, P])
        age_n = sb("age_n", [P, T])
        pop_n = sb("pop_n", [P, T])
        mask_n = sb("mask_n", [P, T], U8)
        maskf = sb("maskf", [P, T])
        decay = sb("decay", [P, T])
        logs_n = sb("logs_n", [P, BLOCKS, J + 1])
        below = sb("below", [P, T])
        u = sb("u", [P, 28])
        (cnt, cnt1, cnt_eps, cnt_min, denom, inv_eps, inv_min, start, inv_denom, pop_sum, age_sum, z1, z2, z, ez,
         e1, gate, omg, large, mean_var0, mean_var1, ln_var, rstd, abs_z, positive, small, gap) = [u[:, n:n + 1] for n in range(27)]
        mean_var = u[:, 19:21]
        row_base = sb("row_base", [P, 1])
        win_w = sb("win_w", [P, WINDOW])
        gate_win = [sb(f"gate_win{s}", [P, WINDOW]) for s in range(TILE_RING)]
        gate_long = [sb(f"gate_long{s}", [P, 1]) for s in range(TILE_RING)]
        row_idx = [sb(f"row_idx{s}", [P, 1], I32) for s in range(TILE_RING)]
        window = sb("window", [P, WINDOW, D])
        user = sb("user", [P, D])
        stats = sb("stats", [P, 6])
        result = sb("result", [P, D])
        ident = sb("ident", [P, P])
        own = sb("own", [P, USERS_PER_CHUNK])
        pick = sb("pick", [P, CHUNKS, USERS_PER_CHUNK])
        times_i = maskf[:, :].bitcast(I32)
        times = sb("times", [P, T])
        base_i = sb("base_i", [P, 1], I32)
        ones8 = sb("ones8", [P, BLOCKS])
        tiny = sb("tiny", [P, 2])
        qk = sb("qk", [P, D])
        wv_t = sb("wv_t", [P, D])
        gamma = sb("gamma", [P, D])
        beta = sb("beta", [P, D])
        gw = sb("gw", [P, 2])
        gb = sb("gb", [P, 1])
        alpha = sb("alpha", [P, 8])
        wq_sb, wk_sb, wv_sb = [products[0][:, n, :] for n in range(3)]

        sums_ps = [ps("sums_ps0"), ps("sums_ps1")]
        query_ps = [ps("query_ps0"), ps("query_ps1")]
        attn_ps = ps("attn_ps")
        turn_ps = ps("turn_ps")
        max_ps = ps("max_ps")
        val_ps = ps("val_ps")
        mean_t_ps = turn_ps[:, 0:GROUP]
        max_t_ps = max_ps[0:CHUNKS, 0:P]
        max_p_ps = max_ps[:, P:P + CHUNKS]
        attended_t_ps = val_ps[:, 0:P]
        long_ps = val_ps[:, P:P + D]

        x_loaded = [[sem(f"x_loaded{s}_{p}") for p in range(PIECES)] for s in range(X_SLOTS)]
        x_free = sem("x_free")
        users_loaded = sem("users_loaded")
        consts_loaded = sem("consts_loaded")
        consts_built = sem("consts_built")
        consts_cast = sem("consts_cast")
        weights_ps = sem("weights_ps")
        weights_ready = sem("weights_ready")
        psum_cleared = sem("psum_cleared")
        alpha_v = sem("alpha_v")
        alpha_a = sem("alpha_a")

        mask_w_ready = sem("mask_w_ready")
        sums_ready = sem("sums_ready")
        sums_copied = sem("sums_copied")
        mean_turned = sem("mean_turned")
        mean_copied = sem("mean_copied")
        query_ready = sem("query_ready")
        query_copied = sem("query_copied")
        products_ready = sem("products_ready")
        scored_a = sem("scored_a")
        scored_v = sem("scored_v")
        logits_scaled = sem("logits_scaled")
        logits_ready = sem("logits_ready")
        maxes_ready = sem("maxes_ready")
        maxes_turned = sem("maxes_turned")
        gmax_ready = sem("gmax_ready")
        gmax_spread = sem("gmax_spread")
        shifted = sem("shifted")
        exps_ready = sem("exps_ready")
        attn_w_ready = sem("attn_w_ready")
        exp_sums_ready = sem("exp_sums_ready")
        attn_sums_ready = sem("attn_sums_ready")
        inv_den_ready = sem("inv_den_ready")
        attended_ready = sem("attended_ready")
        attended_turned = sem("attended_turned")
        attended_copied = sem("attended_copied")
        long_ready = sem("long_ready")

        maskf_ready = sem("maskf_ready")
        age_exp_ready = sem("age_exp_ready")
        decay_ready = sem("decay_ready")
        penalty_ready = sem("penalty_ready")
        log_ready = sem("log_ready")
        logs_summed = sem("logs_summed")
        scale_ready = sem("scale_ready")
        logs_spread = [sem(f"logs_spread{s}") for s in range(TILE_RING)]
        user_counts = sem("user_counts")
        user_derived = sem("user_derived")
        user_windows = sem("user_windows")
        row_idx_ready = sem("row_idx_ready")
        lastk_ready = sem("lastk_ready")
        ctx_sums = sem("ctx_sums")
        gate_chain = sem("gate_chain")
        gate_exp = sem("gate_exp")
        gate_tail = sem("gate_tail")
        gates_ready = sem("gates_ready")
        row_base_moved = sem("row_base_moved")
        window_loaded = sem("window_loaded")
        short_sums = sem("short_sums")
        stats_ready = sem("stats_ready")
        ln_var_ready = sem("ln_var_ready")
        rstd_ready = sem("rstd_ready")
        normed_ready = sem("normed_ready")
        result_ready = sem("result_ready")
        held = {e: sem(f"held_{e}") for e in ("sync", "gpsimd", "vector")}
        stored = sem("stored")

        block = ctx.enter_context(nc.Block())

        def spread_count(k):
            return k.per(TILE_RING).times(16 * 2 * CHUNKS, 16 * 2 * CHUNKS)

        @block.sync
        def _(sp):
            def load_users(k):
                hold(sp, ctx_sums, k.times(2), held["sync"])
                hold(sp, age_exp_ready, k.times(1), held["sync"])
                at = k.times(1)
                sp.dma_start(mask_n[:, :], mask_t[at]).then_inc(users_loaded, 16)
                sp.dma_start(age_n[:, :], age_t[at]).then_inc(users_loaded, 16)
                sp.dma_start(pop_n[:, :], pop_t[at]).then_inc(users_loaded, 16)

            def step(i):
                if i.const % 2 and i.inside(-1, GROUPS - 1):
                    load_users((i + 1).per(2))
                if i.inside(0, GROUPS):
                    for p in range(PIECES):
                        hold(sp, x_free, i.times(PIECES, p + 1 - X_SLOTS * PIECES), held["sync"])
                        sp.dma_start(x[i.const % X_SLOTS][:, :, p * JP:(p + 1) * JP, :].rearrange("p c j d -> p c (j d)"),
                                     items_g[i.times(1)][:, :, p * JP * D:(p + 1) * JP * D])\
                          .then_inc(x_loaded[i.const % X_SLOTS][p], 16)

            run_steps(sp, step, -1, GROUPS - 1)

        @block.gpsimd
        def _(pool):
            nc.gpsimd.memset(ident[:, :], 0.0).then_inc(consts_built, 1)
            nc.gpsimd.memset(pick[:, :, :], 0.0).then_inc(consts_built, 1)
            nc.gpsimd.memset(own[:, :], 1.0).then_inc(consts_built, 1)
            nc.gpsimd.memset(ones8[:, :], 1.0).then_inc(consts_built, 1)
            nc.gpsimd.memset(tiny[:, 0:1], 1e-12).then_inc(consts_built, 1)
            nc.gpsimd.memset(tiny[:, 1:2], 1e-5).then_inc(consts_built, 1)
            nc.gpsimd.iota(times_i, [[1, T]], base=0, channel_multiplier=0).then_inc(consts_built, 1)
            nc.gpsimd.iota(base_i[:, :], [[0, 1]], base=0, channel_multiplier=T).then_inc(consts_built, 1)
            pool.wait_ge(consts_built, 8)
            nc.gpsimd.affine_select(out=ident[:, :], in_=ident[:, :], compare_op=ALU.not_equal, fill=1.0, base=0,
                                    pattern=[[-1, P]], channel_multiplier=1).then_inc(consts_built, 1)
            nc.gpsimd.affine_select(out=pick[:, :, :], in_=pick[:, :, :], compare_op=ALU.not_equal, fill=1.0, base=0,
                                    pattern=[[-STRIP, CHUNKS], [-1, USERS_PER_CHUNK]], channel_multiplier=1)\
                .then_inc(consts_built, 1)
            nc.gpsimd.affine_select(out=own[:, :], in_=own[:, :], compare_op=ALU.is_ge, fill=0.0, base=0,
                                    pattern=[[-BLOCKS, USERS_PER_CHUNK]], channel_multiplier=1).then_inc(consts_built, 1)
            pool.wait_ge(consts_built, 11)
            nc.gpsimd.affine_select(out=own[:, :], in_=own[:, :], compare_op=ALU.is_ge, fill=0.0, base=BLOCKS - 1,
                                    pattern=[[BLOCKS, USERS_PER_CHUNK]], channel_multiplier=-1)\
                .then_inc(consts_built, 1)
            pool.wait_ge(weights_ps, 2)

            def multiply(g, c):
                wait(pool, query_copied, g.times(1, 1))
                wait(pool, scored_a, g.times(CHUNKS, c + 1 - 2))
                nc.gpsimd.tensor_tensor(products[c % 2][:, :, :], x[g.const % X_SLOTS][:, c, SV:J, :],
                                        query_sb[:, c:c + 1, :].to_broadcast([P, SP_, D]), ALU.mult)\
                    .then_inc(products_ready, 1)

            def mask_decay(k):
                kk = k - 1
                if kk.inside(0, TILES):
                    wait(pool, logs_spread[kk.const % TILE_RING], spread_count(kk))
                hold(pool, maskf_ready, k.times(1, 1), held["gpsimd"])
                nc.gpsimd.tensor_scalar(logs_n[:, :, 0:J], maskf[:, :].rearrange("p (t j) -> p t j", t=BLOCKS),
                                        -MASKED, MASKED, ALU.mult, ALU.add)\
                    .then_inc(penalty_ready, 1)
                wait(pool, age_exp_ready, k.times(1, 1))
                nc.gpsimd.tensor_tensor(decay[:, :], decay[:, :], maskf[:, :], ALU.mult).then_inc(decay_ready, 1)

            def sum_logs(k):
                wait(pool, log_ready, k.times(1, 1))
                wait(pool, penalty_ready, k.times(1, 1))
                nc.gpsimd.tensor_tensor(logs_n[:, :, 0:J], decay[:, :].rearrange("p (t j) -> p t j", t=BLOCKS),
                                        logs_n[:, :, 0:J], ALU.add)\
                    .then_inc(logs_summed, 1)

            def fetch_windows(k):
                wait(pool, row_idx_ready, k.times(1, 1))
                hold(pool, short_sums, k.times(WINDOW + 1), held["gpsimd"])
                for w in range(WINDOW):
                    nc.gpsimd.indirect_dma_start(
                        out=window[:, w, :], out_offset=None, in_=rows[:, :],
                        in_offset=bass.IndirectOffsetOnAxis(ap=row_idx[k.const % TILE_RING][:, 0:1], axis=0),
                        element_offset=w * D).then_inc(window_loaded, 16)

            def step(i):
                g, odd = i - 1, i.const % 2 == 1
                score, k = g.inside(0, GROUPS), (i + 1).per(2)
                if odd and ((i - 3).per(2)).inside(0, TILES):
                    fetch_windows((i - 3).per(2))
                if score:
                    multiply(g, 0)
                if odd and k.inside(0, TILES):
                    mask_decay(k)
                if score:
                    multiply(g, 1)
                if odd and k.inside(0, TILES):
                    sum_logs(k)
                if score:
                    multiply(g, 2)
                    multiply(g, 3)

            run_steps(pool, step, -1, GROUPS + 2)

        @block.scalar
        def _(act):
            act.dma_start(wq_sb, Wq).then_inc(consts_loaded, 16)
            act.dma_start(wk_sb, Wk).then_inc(consts_loaded, 16)
            act.dma_start(wv_sb, Wv).then_inc(consts_loaded, 16)
            act.dma_start(alpha[:, 0:1], decay_alpha.to_broadcast([P, 1])).then_inc(consts_loaded, 16)
            act.dma_start(gw[:, :], gate_w.to_broadcast([P, 2])).then_inc(consts_loaded, 16)
            act.dma_start(gb[:, :], gate_b.to_broadcast([P, 1])).then_inc(consts_loaded, 16)
            act.dma_start(gamma[:, :], ln_gamma.to_broadcast([P, D])).then_inc(consts_loaded, 16)
            act.dma_start(beta[:, :], ln_beta.to_broadcast([P, D])).then_inc(consts_loaded, 16)
            act.wait_ge(alpha_v, 2)
            nc.scalar.activation(alpha[:, 3:4], alpha[:, 2:3], ACT.Exp, scale=-1.0).then_inc(alpha_a, 1)
            act.wait_ge(alpha_a, 1)
            nc.scalar.activation(alpha[:, 4:5], alpha[:, 3:4], ACT.Ln, bias=1.0).then_inc(alpha_a, 1)
            act.wait_ge(alpha_v, 5)
            act.wait_ge(consts_built, 6)

            def exp_age(k):
                wait(act, users_loaded, k.times(48, 48))
                wait(act, logs_summed, k.times(1))
                nc.scalar.activation(decay[:, :], age_n[:, :], ACT.Exp, scale=alpha[:, 7:8]).then_inc(age_exp_ready, 1)

            def log_decay(k):
                wait(act, decay_ready, k.times(1, 1))
                nc.scalar.activation(decay[:, :], decay[:, :], ACT.Ln, bias=tiny[:, 0:1]).then_inc(log_ready, 1)

            def spread_logs(k):
                wait(act, logs_summed, k.times(1, 1))
                wait(act, scale_ready, k.times(1, 1))
                for h in range(2):
                    for c in range(CHUNKS):
                        first = (h * CHUNKS + c) * USERS_PER_CHUNK
                        act.dma_start(logs_p[(2 * k.const + h) % UNROLL][:, c, :],
                                      logs_n[first:first + USERS_PER_CHUNK, :, :])\
                           .then_inc(logs_spread[k.const % TILE_RING], 16)

            def exp_gate(k):
                wait(act, gate_chain, k.times(5, 5))
                nc.scalar.activation(ez, abs_z, ACT.Exp, scale=-1.0).then_inc(gate_exp, 1)

            def sum_products(g, c, first, end):
                if first == 0:
                    wait(act, products_ready, g.times(CHUNKS, c + 1))
                for j in range(first, end):
                    ins = nc.scalar.activation(products[c % 2][:, j, :], products[c % 2][:, j, :], ACT.Copy,
                                               accum_out=raw[g.const % 2][:, c, SV + j:SV + j + 1])
                if end == SP_:
                    ins.then_inc(scored_a, 1)

            def exponentials(g):
                wait(act, shifted, g.times(1, 1))
                wait(act, exp_sums_ready, g.times(1))
                wait(act, attn_w_ready, g.times(1))
                nc.scalar.activation(exps[:, :, :], logits[:, :, :], ACT.Exp).then_inc(exps_ready, 1)

            def copy_attended(g):
                wait(act, inv_den_ready, g.times(1, 1))
                wait(act, attended_turned, g.times(1))
                nc.scalar.activation(attended[:, :], attn_ps[:, 0:D], ACT.Copy, scale=inv_den[:, 0:1])\
                    .then_inc(attended_ready, 1)

            def copy_attended_t(k):
                wait(act, attended_turned, k.times(2, 2))
                wait(act, long_ready, k.times(1))
                nc.scalar.activation(attended_t[:, :], attended_t_ps, ACT.Copy).then_inc(attended_copied, 1)

            def copy_sums(g):
                wait(act, sums_ready, g.times(1, 1))
                wait(act, mean_turned, g.times(1))
                nc.scalar.activation(sums_sb[:, :], sums_ps[g.const % 2][:, 0:D], ACT.Copy).then_inc(sums_copied, 1)

            def copy_mean(g):
                wait(act, mean_turned, g.times(1, 1))
                wait(act, query_ready, g.times(1))
                nc.scalar.activation(mean_t[:, :, :], mean_t_ps.rearrange("p (b t) -> p b t", t=1)
                                     .to_broadcast([P, GROUP, BLOCKS]), ACT.Copy).then_inc(mean_copied, 1)

            def copy_query(g):
                wait(act, query_ready, g.times(1, 1))
                wait(act, products_ready, g.times(CHUNKS))
                nc.scalar.activation(query_sb[:, :, :].rearrange("p c d -> p (c d)"), query_ps[g.const % 2][:, :],
                                     ACT.Copy).then_inc(query_copied, 1)

            def inverse_deviation(k):
                wait(act, stats_ready, k.times(2, 2))
                nc.scalar.activation(ln_var, mean_var1, ACT.Ln, bias=tiny[:, 1:2]).then_inc(ln_var_ready, 1)
                wait(act, ln_var_ready, k.times(1, 1))
                nc.scalar.activation(rstd, ln_var, ACT.Exp, scale=-0.5).then_inc(rstd_ready, 1)

            def store(k):
                wait(act, result_ready, k.times(1, 1))
                act.dma_start(out_t[k.times(1)], result[:, :]).then_inc(stored, 16)

            def step(i):
                g, odd = i - 1, i.const % 2 == 1
                score, attend = g.inside(0, GROUPS), (i - 2).inside(0, GROUPS)
                prepare, k = odd and i.inside(-1, GROUPS - 1), (i + 1).per(2)
                finish, kf = not odd and i.inside(4, GROUPS + 4), (i - 4).per(2)
                if odd and (i - 5).inside(0, GROUPS):
                    store((i - 5).per(2))
                if prepare:
                    exp_age(k)
                if score:
                    sum_products(g, 0, 0, SP_)
                if finish:
                    copy_attended_t(kf)
                if prepare:
                    log_decay(k)
                if score:
                    sum_products(g, 1, 0, SP_ // 2)
                if attend:
                    exponentials(i - 2)
                if score:
                    sum_products(g, 1, SP_ // 2, SP_)
                if prepare:
                    spread_logs(k)
                if score:
                    sum_products(g, 2, 0, SP_)
                if prepare:
                    exp_gate(k)
                if score:
                    sum_products(g, 3, 0, SP_)
                if finish:
                    inverse_deviation(kf)
                if attend:
                    copy_attended(i - 2)
                if i.inside(0, GROUPS):
                    copy_sums(i)
                    copy_mean(i)
                    copy_query(i)

            run_steps(act, step, -1, GROUPS + 3)
            act.wait_ge(stored, 16 * TILES)

        @block.tensor
        def _(pe):
            pe.wait_ge(consts_loaded, 16 * 8)
            pe.wait_ge(consts_built, 12)
            pe.matmul(max_ps[:, 0:D], wq_sb, wk_sb, start=True, stop=True).then_inc(weights_ps, 1)
            pe.transpose(val_ps[:, 0:D], wv_sb, ident[:, :]).then_inc(weights_ps, 1)
            pe.wait_ge(weights_ready, 2)
            pe.wait_ge(psum_cleared, 4)

            def masked_sums(g, p):
                if p == 0:
                    wait(pe, mask_w_ready, g.times(1, 1))
                    wait(pe, sums_copied, g.times(1, -1))
                pe.wait_ge(x_loaded[g.const % X_SLOTS][p], g.per(X_SLOTS).times(16, 16))
                for j in range(p * JP, (p + 1) * JP):
                    for c in range(CHUNKS):
                        mm = pe.matmul(sums_ps[g.const % 2][STRIP * c:STRIP * c + USERS_PER_CHUNK, 0:D],
                                       mask_w[g.const % 2][:, c, j, :], x[g.const % X_SLOTS][:, c, j, :],
                                       start=(j == 0), stop=(j == J - 1))
                if p == PIECES - 1:
                    mm.then_inc(sums_ready, 1)

            def queries(g):
                wait(pe, sums_copied, g.times(1, 1))
                pe.matmul(mean_t_ps, sums_sb[:, :], pick[:, :, :].rearrange("p c b -> p (c b)"),
                          start=True, stop=True).then_inc(mean_turned, 1)
                wait(pe, mean_copied, g.times(1, 1))
                wait(pe, scored_v, g.times(2 * CHUNKS, -2 * CHUNKS))
                for c in range(CHUNKS):
                    users = mean_t[:, USERS_PER_CHUNK * c:USERS_PER_CHUNK * (c + 1), :]
                    mm = pe.matmul(query_ps[g.const % 2][:, D * c:D * (c + 1)],
                                   users.rearrange("p b t -> p (b t)"),
                                   qk[:, :], start=True, stop=True)
                mm.then_inc(query_ready, 1)

            def turn_maxes(g):
                wait(pe, maxes_ready, g.times(1, 1))
                pe.transpose(max_t_ps, maxes[:, :], ident[:, :]).then_inc(maxes_turned, 1)

            def spread_gmax(g):
                wait(pe, gmax_ready, g.times(2, 2))
                pe.matmul(max_p_ps, gmax_wide[:, :, :].rearrange("c b t -> c (b t)"),
                          ident[0:CHUNKS, 0:CHUNKS], start=True, stop=True).then_inc(gmax_spread, 1)

            def attention_sums(g, p):
                if p == 0:
                    wait(pe, attn_w_ready, g.times(1, 1))
                    wait(pe, attended_ready, g.times(1))
                for j in range(p * JP, (p + 1) * JP):
                    for c in range(CHUNKS):
                        mm = pe.matmul(attn_ps[STRIP * c:STRIP * c + USERS_PER_CHUNK, 0:D],
                                       attn_w[:, c, j, :], x[g.const % X_SLOTS][:, c, j, :],
                                       start=(j == 0), stop=(j == J - 1))
                mm.then_inc(x_free, 1)
                if p == PIECES - 1:
                    wait(pe, exp_sums_ready, g.times(1, 1))
                    for c in range(CHUNKS):
                        mm = pe.matmul(attn_ps[STRIP * c:STRIP * c + USERS_PER_CHUNK, D:D + 1],
                                       own[:, :], exp_sums[:, c:c + 1], start=True, stop=True)
                    mm.then_inc(attn_sums_ready, 1)

            def turn_attended(g):
                wait(pe, attended_ready, g.times(1, 1))
                wait(pe, attended_copied, g.per(2).times(1))
                wait(pe, short_sums, g.per(2).times(WINDOW + 1))
                h = g.const % 2
                pe.matmul(attended_t_ps[:, GROUP * h:GROUP * (h + 1)], attended[:, :],
                          pick[:, :, :].rearrange("p c b -> p (c b)"), start=True, stop=True)\
                    .then_inc(attended_turned, 1)

            def project_values(k):
                wait(pe, attended_copied, k.times(1, 1))
                pe.matmul(long_ps, attended_t[:, :], wv_t[:, :], start=True, stop=True).then_inc(long_ready, 1)

            def step(i):
                g = i - 2
                load, attend = i.inside(0, GROUPS), g.inside(0, GROUPS)
                if load:
                    masked_sums(i, 0)
                if (i - 3).inside(0, GROUPS):
                    turn_attended(i - 3)
                if attend:
                    turn_maxes(g)
                if load:
                    masked_sums(i, 1)
                if attend:
                    spread_gmax(g)
                if i.const % 2 == 0 and i.inside(4, GROUPS + 4):
                    project_values((i - 4).per(2))
                if attend:
                    attention_sums(g, 0)
                    attention_sums(g, 1)
                if load:
                    masked_sums(i, 2)
                if attend:
                    attention_sums(g, 2)
                    attention_sums(g, 3)
                if load:
                    masked_sums(i, 3)
                if attend:
                    attention_sums(g, 4)
                if load:
                    masked_sums(i, 4)
                    queries(i)

            run_steps(pe, step, 0, GROUPS + 2)

        @block.vector
        def _(dve):
            for bank in (sums_ps[0], sums_ps[1], attn_ps):
                nc.vector.memset(bank[:, :], 0.0).then_inc(psum_cleared, 1)
            dve.wait_ge(psum_cleared, 3)
            nc.vector.memset(attn_ps[:, D:D + 1], 1.0).then_inc(psum_cleared, 1)
            dve.wait_ge(consts_built, 8)
            nc.vector.tensor_copy(times[:, :], times_i).then_inc(consts_cast, 1)
            nc.vector.tensor_copy(row_base[:, :], base_i[:, :]).then_inc(consts_cast, 1)
            dve.wait_ge(consts_loaded, 16 * 8)
            nc.vector.tensor_scalar(alpha[:, 1:2], alpha[:, 0:1], -1.0, None, ALU.mult).then_inc(alpha_v, 1)
            dve.wait_ge(alpha_v, 1)
            nc.vector.tensor_tensor(alpha[:, 2:3], alpha[:, 0:1], alpha[:, 1:2], ALU.max).then_inc(alpha_v, 1)
            nc.vector.tensor_scalar(alpha[:, 5:6], alpha[:, 0:1], 0.0, None, ALU.max).then_inc(alpha_v, 1)
            dve.wait_ge(alpha_v, 3)
            dve.wait_ge(alpha_a, 2)
            nc.vector.tensor_tensor(alpha[:, 6:7], alpha[:, 5:6], alpha[:, 4:5], ALU.add).then_inc(alpha_v, 1)
            dve.wait_ge(alpha_v, 4)
            nc.vector.tensor_scalar(alpha[:, 7:8], alpha[:, 6:7], 1e-6, -1.0, ALU.add, ALU.mult).then_inc(alpha_v, 1)
            dve.wait_ge(weights_ps, 2)
            nc.vector.tensor_copy(qk[:, :], max_ps[:, 0:D]).then_inc(weights_ready, 1)
            nc.vector.tensor_copy(wv_t[:, :], val_ps[:, 0:D]).then_inc(weights_ready, 1)
            dve.wait_ge(consts_cast, 2)

            def build_mask_weights(g):
                k = g.per(2)
                wait(dve, logs_spread[k.const % TILE_RING], spread_count(k))
                wait(dve, sums_ready, g.times(1, -1))
                logs = logs_p[g.const % UNROLL]
                for c in range(CHUNKS):
                    w = nc.vector.scalar_tensor_tensor(
                        out=mask_w[g.const % 2][:, c, :, :],
                        in0=logs[:, c, 0:J].rearrange("p (j b) -> p j b", b=1).to_broadcast([P, J, USERS_PER_CHUNK]),
                        scalar=MASKED / 2,
                        in1=own[:, :].rearrange("p (j b) -> p j b", j=1).to_broadcast([P, J, USERS_PER_CHUNK]),
                        op0=ALU.is_gt, op1=ALU.mult)
                w.then_inc(mask_w_ready, 1)

            def score(g, c, first, end):
                if first == 0 and c == 0:
                    wait(dve, query_copied, g.times(1, 1))
                for j in range(first, end):
                    if j in (0, SV_HALF):
                        wait(dve, scored_v, g.times(2 * CHUNKS, 2 * c - 1 + (j > 0)))
                    ins = nc.vector.tensor_tensor_reduce(
                        unused_v[:, j, :], x[g.const % X_SLOTS][:, c, j, :], query_ps[g.const % 2][:, D * c:D * (c + 1)],
                        1.0, 0.0, ALU.mult, ALU.add, raw[g.const % 2][:, c, j:j + 1])
                    if j in (SV_HALF - 1, SV - 1):
                        ins.then_inc(scored_v, 1)

            def scale_logits(g):
                wait(dve, scored_a, g.times(CHUNKS, CHUNKS))
                wait(dve, scored_v, g.times(2 * CHUNKS, 2 * CHUNKS))
                wait(dve, exps_ready, g.times(1))
                logs = logs_p[g.const % UNROLL]
                nc.vector.tensor_tensor(logits[:, :, :], raw[g.const % 2][:, :, :],
                                        logs[:, :, J:J + 1].to_broadcast([P, CHUNKS, J]), ALU.mult)\
                    .then_inc(logits_scaled, 1)

            def add_logs(g):
                wait(dve, logits_scaled, g.times(1, 1))
                nc.vector.tensor_tensor(logits[:, :, :], logits[:, :, :], logs_p[g.const % UNROLL][:, :, 0:J], ALU.add)\
                    .then_inc(logits_ready, 1)

            def partition_maxes(g):
                wait(dve, logits_ready, g.times(1, 1))
                nc.vector.tensor_reduce(maxes[:, :], logits[:, :, :], AX_X, ALU.max).then_inc(maxes_ready, 1)

            def user_maxes(g):
                wait(dve, maxes_turned, g.times(1, 1))
                nc.vector.tensor_reduce(gmax[:, :], max_t_ps.rearrange("c (b t) -> c b t", t=BLOCKS), AX_X, ALU.max)\
                    .then_inc(gmax_ready, 1)

            def widen_maxes(g):
                wait(dve, gmax_ready, g.times(2, 1))
                nc.vector.tensor_copy(gmax_wide[:, :, :], gmax[:, :].rearrange("c (b t) -> c b t", t=1)
                                      .to_broadcast([CHUNKS, USERS_PER_CHUNK, BLOCKS])).then_inc(gmax_ready, 1)

            def shift(g):
                wait(dve, gmax_spread, g.times(1, 1))
                nc.vector.tensor_tensor(logits[:, :, :], logits[:, :, :],
                                        max_p_ps.rearrange("p (c j) -> p c j", j=1).to_broadcast([P, CHUNKS, J]),
                                        ALU.subtract).then_inc(shifted, 1)

            def build_attention_weights(g):
                wait(dve, exps_ready, g.times(1, 1))
                wait(dve, x_free, g.times(PIECES))
                for c in range(CHUNKS):
                    w = nc.vector.tensor_tensor(
                        attn_w[:, c, :, :],
                        exps[:, c, :].rearrange("p (j b) -> p j b", b=1).to_broadcast([P, J, USERS_PER_CHUNK]),
                        own[:, :].rearrange("p (j b) -> p j b", j=1).to_broadcast([P, J, USERS_PER_CHUNK]), ALU.mult)
                w.then_inc(attn_w_ready, 1)
                wait(dve, attn_sums_ready, g.times(1))
                nc.vector.tensor_reduce(exp_sums[:, :], exps[:, :, :], AX_X, ALU.add).then_inc(exp_sums_ready, 1)

            def invert_denominators(g):
                wait(dve, attn_sums_ready, g.times(1, 1))
                wait(dve, attended_ready, g.times(1))
                nc.vector.reciprocal(inv_den[:, :], attn_ps[:, D:D + 1]).then_inc(inv_den_ready, 1)

            def count_masks(k):
                wait(dve, users_loaded, k.times(48, 48))
                wait(dve, decay_ready, k.times(1))
                wait(dve, penalty_ready, k.times(1))
                nc.vector.tensor_scalar(maskf[:, :], mask_n[:, :], 1.0, None, ALU.mult, ALU.add, accum_out=cnt)\
                    .then_inc(maskf_ready, 1)

            def bound_counts(k):
                wait(dve, maskf_ready, k.times(1, 1))
                nc.vector.tensor_scalar(cnt1, cnt, 1.0, None, ALU.max).then_inc(user_counts, 1)
                nc.vector.tensor_scalar(cnt_eps, cnt, 1e-6, None, ALU.add).then_inc(user_counts, 1)
                nc.vector.tensor_scalar(cnt_min, cnt, 1.0, None, ALU.min).then_inc(user_counts, 1)

            def invert_counts(k):
                wait(dve, user_counts, k.times(3, 3))
                nc.vector.tensor_scalar(denom, cnt1, float(WINDOW), None, ALU.min).then_inc(user_derived, 1)
                nc.vector.reciprocal(inv_eps, cnt_eps).then_inc(user_derived, 1)
                nc.vector.reciprocal(inv_min, cnt_min).then_inc(user_derived, 1)
                nc.vector.tensor_scalar(below[:, :], times[:, :], cnt1, None, ALU.is_lt).then_inc(user_windows, 1)

            def place_windows(k):
                wait(dve, user_derived, k.times(3, 3))
                nc.vector.tensor_tensor(start, cnt1, denom, ALU.subtract).then_inc(user_windows, 1)
                nc.vector.reciprocal(inv_denom, denom).then_inc(user_windows, 1)
                kk = k - 1
                if kk.inside(0, TILES):
                    wait(dve, logs_spread[kk.const % TILE_RING], spread_count(kk))
                nc.vector.tensor_scalar(logs_n[:, :, J], ones8[:, :], inv_eps, SCALE, ALU.mult, ALU.mult)\
                    .then_inc(scale_ready, 1)

            def window_weights(k):
                wait(dve, user_windows, k.times(4, 3))
                wait(dve, row_base_moved, k.times(1))
                nc.vector.tensor_tensor(row_idx[k.const % TILE_RING][:, :], start, row_base[:, :], ALU.add)\
                    .then_inc(row_idx_ready, 1)
                nc.vector.tensor_scalar(win_w[:, :], times[:, 0:WINDOW], denom, inv_denom, ALU.is_lt, ALU.mult)\
                    .then_inc(user_windows, 1)
                nc.vector.scalar_tensor_tensor(out=below[:, :], in0=times[:, :], scalar=start, in1=below[:, :],
                                               op0=ALU.is_ge, op1=ALU.mult).then_inc(lastk_ready, 1)

            def window_sums(k):
                wait(dve, row_idx_ready, k.times(1, 1))
                nc.vector.tensor_scalar(row_base[:, :], row_base[:, :], float(P * T), None, ALU.add)\
                    .then_inc(row_base_moved, 1)
                wait(dve, lastk_ready, k.times(1, 1))
                nc.vector.tensor_tensor_reduce(pop_n[:, :], pop_n[:, :], below[:, :], 1.0, 0.0, ALU.mult, ALU.add,
                                               pop_sum).then_inc(ctx_sums, 1)
                wait(dve, age_exp_ready, k.times(1, 1))
                nc.vector.tensor_tensor_reduce(age_n[:, :], age_n[:, :], below[:, :], 1.0, 0.0, ALU.mult, ALU.add,
                                               age_sum).then_inc(ctx_sums, 1)

            def gate_logit_pop(k):
                wait(dve, ctx_sums, k.times(2, 2))
                nc.vector.tensor_scalar(z1, pop_sum, gw[:, 0:1], None, ALU.mult).then_inc(gate_chain, 1)

            def gate_logit_age(k):
                wait(dve, gate_chain, k.times(5, 1))
                nc.vector.scalar_tensor_tensor(out=z2, in0=age_sum, scalar=gw[:, 1:2], in1=z1, op0=ALU.mult,
                                               op1=ALU.add).then_inc(gate_chain, 1)

            def gate_logit(k):
                wait(dve, gate_chain, k.times(5, 2))
                nc.vector.tensor_scalar(z, z2, inv_denom, gb[:, 0:1], ALU.mult, ALU.add).then_inc(gate_chain, 1)

            def gate_magnitude(k):
                wait(dve, gate_chain, k.times(5, 3))
                nc.vector.scalar_tensor_tensor(out=abs_z, in0=z, scalar=-1.0, in1=z, op0=ALU.mult, op1=ALU.max)\
                    .then_inc(gate_chain, 1)
                nc.vector.tensor_scalar(positive, z, 0.0, None, ALU.is_ge).then_inc(gate_chain, 1)

            def gate_denominator(k):
                wait(dve, gate_exp, k.times(1, 1))
                nc.vector.tensor_scalar(e1, ez, 1.0, None, ALU.add).then_inc(gate_tail, 1)

            def gate_large(k):
                wait(dve, gate_tail, k.times(6, 1))
                nc.vector.reciprocal(large, e1).then_inc(gate_tail, 1)

            def gate_small(k):
                wait(dve, gate_tail, k.times(6, 2))
                nc.vector.tensor_tensor(small, ez, large, ALU.mult).then_inc(gate_tail, 1)

            def gate_gap(k):
                wait(dve, gate_tail, k.times(6, 3))
                nc.vector.tensor_tensor(gap, large, small, ALU.subtract).then_inc(gate_tail, 1)

            def gate_value(k):
                wait(dve, gate_tail, k.times(6, 4))
                nc.vector.scalar_tensor_tensor(out=gate, in0=gap, scalar=positive, in1=small, op0=ALU.mult,
                                               op1=ALU.add).then_inc(gate_tail, 1)

            def gate_rest(k):
                wait(dve, gate_tail, k.times(6, 5))
                nc.vector.tensor_scalar(omg, gate, -1.0, 1.0, ALU.mult, ALU.add).then_inc(gate_tail, 1)

            def gate_weights(k):
                wait(dve, user_windows, k.times(4, 4))
                nc.vector.tensor_scalar(gate_win[k.const % TILE_RING][:, :], win_w[:, :], gate, None, ALU.mult)\
                    .then_inc(gates_ready, 1)
                wait(dve, gate_tail, k.times(6, 6))
                nc.vector.tensor_tensor(gate_long[k.const % TILE_RING][:, :], omg, inv_min, ALU.mult)\
                    .then_inc(gates_ready, 1)

            def short_term(k, w):
                if w == 0:
                    wait(dve, window_loaded, k.times(16 * WINDOW, 16 * WINDOW))
                    wait(dve, gates_ready, k.times(2, 2))
                    nc.vector.tensor_scalar(user[:, :], window[:, 0, :], gate_win[k.const % TILE_RING][:, 0:1], None,
                                            ALU.mult).then_inc(short_sums, 1)
                else:
                    wait(dve, short_sums, k.times(WINDOW + 1, w))
                    nc.vector.scalar_tensor_tensor(out=user[:, :], in0=window[:, w, :],
                                                   scalar=gate_win[k.const % TILE_RING][:, w:w + 1], in1=user[:, :],
                                                   op0=ALU.mult, op1=ALU.add).then_inc(short_sums, 1)

            def add_long_term(k):
                wait(dve, long_ready, k.times(1, 1))
                wait(dve, short_sums, k.times(WINDOW + 1, WINDOW))
                nc.vector.scalar_tensor_tensor(out=user[:, :], in0=long_ps, scalar=gate_long[k.const % TILE_RING][:, 0:1],
                                               in1=user[:, :], op0=ALU.mult, op1=ALU.add).then_inc(short_sums, 1)

            def measure(k):
                wait(dve, short_sums, k.times(WINDOW + 1, WINDOW + 1))
                nc.vector.bn_stats(stats[:, :], user[:, :]).then_inc(stats_ready, 1)

            def measure_all(k):
                hold(dve, stats_ready, k.times(2, 1), held["vector"])
                nc.vector.bn_aggr(mean_var, stats[:, :]).then_inc(stats_ready, 1)

            def normalise(k):
                wait(dve, rstd_ready, k.times(1, 1))
                wait(dve, stored, k.times(16))
                nc.vector.tensor_scalar(result[:, :], user[:, :], mean_var0, rstd, ALU.subtract, ALU.mult)\
                    .then_inc(normed_ready, 1)

            def scale_normed(k):
                wait(dve, normed_ready, k.times(2, 1))
                nc.vector.tensor_tensor(result[:, :], result[:, :], gamma[:, :], ALU.mult).then_inc(normed_ready, 1)

            def add_beta(k):
                wait(dve, normed_ready, k.times(2, 2))
                nc.vector.tensor_tensor(result[:, :], result[:, :], beta[:, :], ALU.add).then_inc(result_ready, 1)

            def step(i):
                g, d, odd = i - 1, i - 2, i.const % 2 == 1
                scoring, attend = g.inside(0, GROUPS), d.inside(0, GROUPS)
                prepare, k = odd and i.inside(-1, GROUPS - 1), (i + 1).per(2)
                finish, kf = not odd and i.inside(4, GROUPS + 4), (i - 4).per(2)

                def part(c, first, end):
                    if scoring:
                        score(g, c, first, end)

                if prepare:
                    count_masks(k)
                part(0, 0, 4)
                if attend:
                    scale_logits(d)
                if prepare:
                    bound_counts(k)
                part(0, 4, 6)
                if attend:
                    add_logs(d)
                if prepare:
                    invert_counts(k)
                part(0, 6, 8)
                if attend:
                    partition_maxes(d)
                if prepare:
                    place_windows(k)
                part(0, 8, 11)
                if attend:
                    user_maxes(d)
                part(0, 11, SV)
                if attend:
                    widen_maxes(d)
                if prepare:
                    window_weights(k)
                if finish:
                    short_term(kf, 0)
                part(1, 0, 5)
                if attend:
                    shift(d)
                if prepare:
                    window_sums(k)
                if finish:
                    short_term(kf, 1)
                part(1, 5, 10)
                if attend:
                    build_attention_weights(d)
                if prepare:
                    gate_logit_pop(k)
                if finish:
                    short_term(kf, 2)
                part(1, 10, SV)
                if prepare:
                    gate_logit_age(k)
                if finish:
                    short_term(kf, 3)
                part(2, 0, 3)
                if prepare:
                    gate_logit(k)
                if finish:
                    short_term(kf, 4)
                part(2, 3, 6)
                if prepare:
                    gate_magnitude(k)
                if finish:
                    add_long_term(kf)
                part(2, 6, 10)
                if finish:
                    measure(kf)
                part(2, 10, SV)
                if finish:
                    measure_all(kf)
                if prepare:
                    gate_denominator(k)
                if (i + 1).inside(0, GROUPS):
                    build_mask_weights(i + 1)
                if prepare:
                    gate_large(k)
                part(3, 0, 3)
                if prepare:
                    gate_small(k)
                part(3, 3, 6)
                if prepare:
                    gate_gap(k)
                part(3, 6, 8)
                if prepare:
                    gate_value(k)
                part(3, 8, 10)
                if prepare:
                    gate_rest(k)
                part(3, 10, SV)
                if prepare:
                    gate_weights(k)
                if finish:
                    normalise(kf)
                if attend:
                    invert_denominators(d)
                if finish:
                    scale_normed(kf)
                    add_beta(kf)

            run_steps(dve, step, -1, GROUPS + 2)


_INS = ["r_hist_items", "r_hist_mask", "r_hist_age_hours", "r_hist_popularity", "L0_rec_Wq", "L0_rec_Wk",
        "L0_rec_Wv", "L0_rec_gate_w", "L0_rec_gate_b", "L0_rec_ln_gamma", "L0_rec_ln_beta", "L0_rec_decay_alpha"]


def kernel(**inputs):
    import numpy as np
    import concourse.bacc as bacc
    from concourse.bass_utils import run_bass_kernel_spmd

    nc = bacc.Bacc("TRN2", target_bir_lowering=False, num_devices=1)
    arrays, args = {}, []
    for name in _INS:
        a = np.ascontiguousarray(inputs[name])
        if a.ndim < 2:
            a = a.reshape(1, -1)
        arrays[f"in_{name}_dram"] = a
        args.append(nc.dram_tensor(f"in_{name}_dram", a.shape, mybir.dt.from_np(a.dtype), kind="ExternalInput").ap())
    users, _, dims = inputs["r_hist_items"].shape
    out = nc.dram_tensor("out_0_dram", (users, dims), F32, kind="ExternalOutput").ap()
    build(nc, *args, out)
    r = run_bass_kernel_spmd(nc, [arrays], core_ids=[0])
    return r.results[0]["out_0_dram"]
```

```python
from contextlib import ExitStack

import concourse.bass as bass
from concourse import mybir

F32 = mybir.dt.float32
BF16 = mybir.dt.bfloat16
I32 = mybir.dt.int32
U8 = mybir.dt.uint8
ALU = mybir.AluOpType
ACT = mybir.ActivationFunctionType
AX_X = mybir.AxisListType.X

P = 128
USERS_PER_CHUNK = 16
CHUNKS = 4
PAIR = 2
STRIP = P // CHUNKS
GROUP = USERS_PER_CHUNK * CHUNKS
BLOCKS = P // USERS_PER_CHUNK
WINDOW = 5
X_SLOTS = 3
UNROLL = 6
TILE_RING = UNROLL // 2
FIRST_LOOP, LOOPS = 5, 4
MASKED = -1.0e30
HALVES = 2
SV = 13

SV_HALF = (SV + 1) // 2


class Step:

    def __init__(self, const, it=None, stride=UNROLL):
        self.const, self.it, self.stride = const, it, stride

    def __add__(self, n):
        return Step(self.const + n, self.it, self.stride)

    def __sub__(self, n):
        return self + -n

    def per(self, n):
        return Step(self.const // n, self.it, self.stride // n)

    def times(self, factor, plus=0):
        if self.it is None:
            return factor * self.const + plus
        return self.it * (factor * self.stride) + (factor * self.const + plus)

    def inside(self, first, end):
        return self.it is not None or first <= self.const < end


def wait(eng, sem, value):
    if not isinstance(value, int) or value > 0:
        eng.wait_ge(sem, value)


def hold(eng, sem, value, held):
    wait(eng, sem, value)
    eng.sem_inc(held, 1)


def run_steps(eng, step, first, last):
    for i in range(first, FIRST_LOOP):
        step(Step(i))
    with eng.Fori(0, LOOPS) as it:
        for u in range(UNROLL):
            step(Step(FIRST_LOOP + u, it))
    for i in range(FIRST_LOOP + UNROLL * LOOPS, last + 1):
        step(Step(i))


def build(nc, items, mask, age, popularity, Wq, Wk, Wv, gate_w, gate_b, ln_gamma, ln_beta, decay_alpha, out):
    USERS, T, D = items.shape
    J = T // BLOCKS
    HALF = [0, (J + 1) // 2, J]
    GROUPS = USERS // GROUP
    TILES = USERS // P
    SP_ = J - SV
    SCALE = 1.0 / float(D) ** 0.5
    assert D == P and GROUPS >= FIRST_LOOP + UNROLL * LOOPS

    items_g = items.rearrange("(g c b) (t j) d -> g (b t) c (j d)", c=CHUNKS, b=USERS_PER_CHUNK, t=BLOCKS)
    rows = items.rearrange("u t d -> (u t) d")
    age_t = age.rearrange("(k p) t -> k p t", p=P)
    pop_t = popularity.rearrange("(k p) t -> k p t", p=P)
    mask_t = mask.rearrange("(k p) t -> k p t", p=P)
    out_t = out.rearrange("(k p) d -> k p d", p=P)

    ctx = ExitStack()
    with ctx:
        def sb(name, shape, dt=F32):
            return ctx.enter_context(nc.sbuf_tensor(name, shape, dt))

        def ps(name):
            return ctx.enter_context(nc.psum_tensor(name, [P, 512], F32))

        def sem(name):
            return ctx.enter_context(nc.semaphore(name))

        x = [sb(f"x{s}", [P, CHUNKS, J, D]) for s in range(X_SLOTS)]
        products = [sb(f"products{s}", [P, SP_, D]) for s in range(2)]
        mask_w = [sb(f"mask_w{s}", [P, CHUNKS, J, USERS_PER_CHUNK]) for s in range(2)]
        attn_w = sb("attn_w", [P, CHUNKS, J, USERS_PER_CHUNK])
        query_sb = [sb(f"query_sb{h}", [P, PAIR, D]) for h in range(2)]
        unused_v = sb("unused_v", [P, SV, D], BF16)
        logs_p = [sb(f"logs_p{s}", [P, CHUNKS, J + 1]) for s in range(UNROLL)]
        raw = [sb(f"raw{s}", [P, CHUNKS, J]) for s in range(2)]
        logits = sb("logits", [P, CHUNKS, J])
        exps = sb("exps", [P, CHUNKS, J])
        maxes = sb("maxes", [P, CHUNKS])
        gmax = sb("gmax", [CHUNKS, USERS_PER_CHUNK])
        gmax_wide = sb("gmax_wide", [CHUNKS, USERS_PER_CHUNK, BLOCKS])
        exp_sums = sb("exp_sums", [P, CHUNKS])
        sums_sb = sb("sums_sb", [P, D])
        mean_t = sb("mean_t", [P, PAIR * USERS_PER_CHUNK, BLOCKS])
        inv_den = sb("inv_den", [P, 2])
        attended = sb("attended", [P, 2, D])
        attended_t = sb("attended_t", [P, P])
        age_n = sb("age_n", [P, T])
        pop_n = sb("pop_n", [P, T])
        mask_n = sb("mask_n", [P, T], U8)
        maskf = sb("maskf", [P, T])
        decay = sb("decay", [P, T])
        logs_n = sb("logs_n", [P, BLOCKS, J + 1])
        below = sb("below", [P, T])
        u = sb("u", [P, 28])
        (cnt, cnt1, cnt_eps, cnt_min, denom, inv_eps, inv_min, start, inv_denom, pop_sum, age_sum, z1, z2, z, ez,
         e1, gate, omg, large, mean_var0, mean_var1, ln_var, rstd, abs_z, positive, small, gap) = [u[:, n:n + 1] for n in range(27)]
        mean_var = u[:, 19:21]
        row_base = sb("row_base", [P, 1])
        win_w = sb("win_w", [P, WINDOW])
        gate_win = [sb(f"gate_win{s}", [P, WINDOW]) for s in range(TILE_RING)]
        gate_long = [sb(f"gate_long{s}", [P, 1]) for s in range(TILE_RING)]
        row_idx = [sb(f"row_idx{s}", [P, 1], I32) for s in range(TILE_RING)]
        window = sb("window", [P, WINDOW, D])
        user = sb("user", [P, D])
        stats = sb("stats", [P, 6])
        result = sb("result", [P, D])
        ident = sb("ident", [P, P])
        own = sb("own", [P, USERS_PER_CHUNK])
        pick = sb("pick", [P, PAIR, USERS_PER_CHUNK])
        times_i = maskf[:, :].bitcast(I32)
        times = sb("times", [P, T])
        base_i = sb("base_i", [P, 1], I32)
        ones8 = sb("ones8", [P, BLOCKS])
        tiny = sb("tiny", [P, 2])
        qk = sb("qk", [P, D])
        wv_t = sb("wv_t", [P, D])
        gamma = sb("gamma", [P, D])
        beta = sb("beta", [P, D])
        gw = sb("gw", [P, 2])
        gb = sb("gb", [P, 1])
        alpha = sb("alpha", [P, 8])
        wq_sb, wk_sb, wv_sb = [products[0][:, n, :] for n in range(3)]

        sums_ps = [ps("sums_ps0"), ps("sums_ps1")]
        query_ps = [ps("query_ps0"), ps("query_ps1")]
        attn_ps = ps("attn_ps")
        turn_ps = ps("turn_ps")
        max_ps = ps("max_ps")
        val_ps = ps("val_ps")
        dens_ps = attn_ps[:, 0:PAIR * (D + 1)].rearrange("p (h w) -> p h w", h=PAIR)[:, :, D]
        mean_t_ps = turn_ps[:, 0:PAIR * USERS_PER_CHUNK]
        max_t_ps = max_ps[0:CHUNKS, 0:P]
        max_p_ps = max_ps[:, P:P + CHUNKS]
        attended_t_ps = val_ps[:, 0:P]
        long_ps = max_ps[:, P + CHUNKS:P + CHUNKS + D]

        x_loaded = [[sem(f"x_loaded{s}_{n}") for n in range(2 * HALVES)] for s in range(X_SLOTS)]
        x_free = sem("x_free")
        users_loaded = sem("users_loaded")
        consts_loaded = sem("consts_loaded")
        consts_built = sem("consts_built")
        consts_cast = sem("consts_cast")
        weights_ps = sem("weights_ps")
        weights_ready = sem("weights_ready")
        psum_cleared = sem("psum_cleared")
        alpha_v = sem("alpha_v")
        alpha_a = sem("alpha_a")

        mask_w_ready = sem("mask_w_ready")
        sums_ready = sem("sums_ready")
        sums_copied = sem("sums_copied")
        mean_turned = sem("mean_turned")
        mean_copied = sem("mean_copied")
        query_ready = sem("query_ready")
        query_copied = sem("query_copied")
        products_ready = sem("products_ready")
        scored_a = sem("scored_a")
        scored_v = sem("scored_v")
        logits_scaled = sem("logits_scaled")
        logits_ready = sem("logits_ready")
        maxes_ready = sem("maxes_ready")
        maxes_turned = sem("maxes_turned")
        gmax_ready = sem("gmax_ready")
        gmax_spread = sem("gmax_spread")
        shifted = sem("shifted")
        exps_ready = sem("exps_ready")
        attn_w_ready = sem("attn_w_ready")
        exp_sums_ready = sem("exp_sums_ready")
        attn_sums_ready = sem("attn_sums_ready")
        inv_den_ready = sem("inv_den_ready")
        attended_ready = sem("attended_ready")
        attended_turned = sem("attended_turned")
        attended_copied = sem("attended_copied")
        long_ready = sem("long_ready")

        maskf_ready = sem("maskf_ready")
        age_exp_ready = sem("age_exp_ready")
        decay_ready = sem("decay_ready")
        penalty_ready = sem("penalty_ready")
        log_ready = sem("log_ready")
        logs_summed = sem("logs_summed")
        scale_ready = sem("scale_ready")
        logs_spread = [sem(f"logs_spread{s}") for s in range(TILE_RING)]
        user_counts = sem("user_counts")
        user_derived = sem("user_derived")
        user_windows = sem("user_windows")
        row_idx_ready = sem("row_idx_ready")
        lastk_ready = sem("lastk_ready")
        ctx_sums = sem("ctx_sums")
        gate_chain = sem("gate_chain")
        gate_exp = sem("gate_exp")
        gate_tail = sem("gate_tail")
        gates_ready = sem("gates_ready")
        row_base_moved = sem("row_base_moved")
        window_loaded = sem("window_loaded")
        short_sums = sem("short_sums")
        stats_ready = sem("stats_ready")
        ln_var_ready = sem("ln_var_ready")
        rstd_ready = sem("rstd_ready")
        normed_ready = sem("normed_ready")
        result_ready = sem("result_ready")
        held = {e: sem(f"held_{e}") for e in ("sync", "gpsimd", "vector")}
        stored = sem("stored")

        block = ctx.enter_context(nc.Block())

        def spread_count(k):
            return k.per(TILE_RING).times(16 * 2 * CHUNKS, 16 * 2 * CHUNKS)

        @block.sync
        def _(sp):
            def load_users(k):
                hold(sp, ctx_sums, k.times(2), held["sync"])
                hold(sp, age_exp_ready, k.times(1), held["sync"])
                at = k.times(1)
                sp.dma_start(mask_n[:, :], mask_t[at]).then_inc(users_loaded, 16)
                sp.dma_start(age_n[:, :], age_t[at]).then_inc(users_loaded, 16)
                sp.dma_start(pop_n[:, :], pop_t[at]).then_inc(users_loaded, 16)

            def load_rows(g, h):
                hold(sp, x_free, g.times(2, h + 1 - 2 * X_SLOTS), held["sync"])
                for q in range(HALVES):
                    sp.dma_start(x[g.const % X_SLOTS][:, PAIR * h:PAIR * (h + 1), HALF[q]:HALF[q + 1], :]
                                 .rearrange("p c j d -> p c (j d)"),
                                 items_g[g.times(1)][:, PAIR * h:PAIR * (h + 1), HALF[q] * D:HALF[q + 1] * D])\
                      .then_inc(x_loaded[g.const % X_SLOTS][HALVES * h + q], 16)

            def spread_logs(k):
                hold(sp, logs_summed, k.times(1, 1), held["sync"])
                hold(sp, scale_ready, k.times(1, 1), held["sync"])
                for h in range(2):
                    for c in range(CHUNKS):
                        first = (h * CHUNKS + c) * USERS_PER_CHUNK
                        sp.dma_start(logs_p[(2 * k.const + h) % UNROLL][:, c, :],
                                     logs_n[first:first + USERS_PER_CHUNK, :, :])\
                          .then_inc(logs_spread[k.const % TILE_RING], 16)

            def step(i):
                if i.const % 2 == 0 and i.inside(-2, GROUPS - 2):
                    load_users((i + 2).per(2))
                if i.inside(0, GROUPS):
                    load_rows(i, 0)
                    load_rows(i, 1)
                if i.const % 2 == 0 and i.inside(-2, GROUPS - 2):
                    spread_logs((i + 2).per(2))

            run_steps(sp, step, -2, GROUPS - 1)

        @block.gpsimd
        def _(pool):
            nc.gpsimd.memset(ident[:, :], 0.0).then_inc(consts_built, 1)
            nc.gpsimd.memset(pick[:, :, :], 0.0).then_inc(consts_built, 1)
            nc.gpsimd.memset(own[:, :], 1.0).then_inc(consts_built, 1)
            nc.gpsimd.memset(ones8[:, :], 1.0).then_inc(consts_built, 1)
            nc.gpsimd.memset(tiny[:, 0:1], 1e-12).then_inc(consts_built, 1)
            nc.gpsimd.memset(tiny[:, 1:2], 1e-5).then_inc(consts_built, 1)
            nc.gpsimd.iota(times_i, [[1, T]], base=0, channel_multiplier=0).then_inc(consts_built, 1)
            nc.gpsimd.iota(base_i[:, :], [[0, 1]], base=0, channel_multiplier=T).then_inc(consts_built, 1)
            pool.wait_ge(consts_built, 8)
            nc.gpsimd.affine_select(out=ident[:, :], in_=ident[:, :], compare_op=ALU.not_equal, fill=1.0, base=0,
                                    pattern=[[-1, P]], channel_multiplier=1).then_inc(consts_built, 1)
            nc.gpsimd.affine_select(out=own[:, :], in_=own[:, :], compare_op=ALU.is_ge, fill=0.0, base=0,
                                    pattern=[[-BLOCKS, USERS_PER_CHUNK]], channel_multiplier=1).then_inc(consts_built, 1)
            nc.gpsimd.affine_select(out=pick[:, :, :], in_=pick[:, :, :], compare_op=ALU.not_equal, fill=1.0, base=0,
                                    pattern=[[-2 * STRIP, PAIR], [-1, USERS_PER_CHUNK]], channel_multiplier=1)\
                .then_inc(consts_built, 1)
            pool.wait_ge(consts_built, 11)
            nc.gpsimd.affine_select(out=pick[:, :, :], in_=pick[:, :, :], compare_op=ALU.not_equal, fill=1.0,
                                    base=-STRIP, pattern=[[-2 * STRIP, PAIR], [-1, USERS_PER_CHUNK]],
                                    channel_multiplier=1).then_inc(consts_built, 1)
            nc.gpsimd.affine_select(out=own[:, :], in_=own[:, :], compare_op=ALU.is_ge, fill=0.0, base=BLOCKS - 1,
                                    pattern=[[BLOCKS, USERS_PER_CHUNK]], channel_multiplier=-1)\
                .then_inc(consts_built, 1)
            pool.wait_ge(weights_ps, 2)

            def multiply(g, c):
                wait(pool, query_copied, g.times(2, c // PAIR + 1))
                wait(pool, scored_a, g.times(CHUNKS, c + 1 - 2))
                nc.gpsimd.tensor_tensor(products[c % 2][:, :, :], x[g.const % X_SLOTS][:, c, SV:J, :],
                                        query_sb[c // PAIR][:, c % PAIR:c % PAIR + 1, :].to_broadcast([P, SP_, D]), ALU.mult)\
                    .then_inc(products_ready, 1)

            def mask_decay(k):
                kk = k - 1
                if kk.inside(0, TILES):
                    wait(pool, logs_spread[kk.const % TILE_RING], spread_count(kk))
                hold(pool, maskf_ready, k.times(1, 1), held["gpsimd"])
                nc.gpsimd.tensor_scalar(logs_n[:, :, 0:J], maskf[:, :].rearrange("p (t j) -> p t j", t=BLOCKS),
                                        -MASKED, MASKED, ALU.mult, ALU.add)\
                    .then_inc(penalty_ready, 1)
                wait(pool, age_exp_ready, k.times(1, 1))
                nc.gpsimd.tensor_tensor(decay[:, :], decay[:, :], maskf[:, :], ALU.mult).then_inc(decay_ready, 1)

            def sum_logs(k):
                wait(pool, log_ready, k.times(1, 1))
                wait(pool, penalty_ready, k.times(1, 1))
                nc.gpsimd.tensor_tensor(logs_n[:, :, 0:J], decay[:, :].rearrange("p (t j) -> p t j", t=BLOCKS),
                                        logs_n[:, :, 0:J], ALU.add)\
                    .then_inc(logs_summed, 1)

            def fetch_windows(k, first, end):
                if first == 0:
                    wait(pool, row_idx_ready, k.times(1, 1))
                    hold(pool, short_sums, k.times(WINDOW + 1), held["gpsimd"])
                for w in range(first, end):
                    nc.gpsimd.indirect_dma_start(
                        out=window[:, w, :], out_offset=None, in_=rows[:, :],
                        in_offset=bass.IndirectOffsetOnAxis(ap=row_idx[k.const % TILE_RING][:, 0:1], axis=0),
                        element_offset=w * D).then_inc(window_loaded, 16)

            def step(i):
                even, odd = i.const % 2 == 0, i.const % 2 == 1
                fetch, kf = even and i.inside(4, GROUPS + 4), (i - 4).per(2)
                if even and i.inside(-2, GROUPS - 2):
                    sum_logs((i + 2).per(2))
                if (i - 1).inside(0, GROUPS):
                    multiply(i - 1, 2)
                if fetch:
                    fetch_windows(kf, 0, 2)
                if (i - 1).inside(0, GROUPS):
                    multiply(i - 1, 3)
                if fetch:
                    fetch_windows(kf, 2, 4)
                if i.inside(0, GROUPS):
                    multiply(i, 0)
                if odd and i.inside(-3, GROUPS - 3):
                    mask_decay((i + 3).per(2))
                if fetch:
                    fetch_windows(kf, 4, WINDOW)
                if i.inside(0, GROUPS):
                    multiply(i, 1)

            run_steps(pool, step, -3, GROUPS + 2)

        @block.scalar
        def _(act):
            nc.scalar.preload_act_table_set("natural_log_exp_and_others")
            act.dma_start(wq_sb, Wq).then_inc(consts_loaded, 16)
            act.dma_start(wk_sb, Wk).then_inc(consts_loaded, 16)
            act.dma_start(wv_sb, Wv).then_inc(consts_loaded, 16)
            act.dma_start(alpha[:, 0:1], decay_alpha.to_broadcast([P, 1])).then_inc(consts_loaded, 16)
            act.dma_start(gw[:, :], gate_w.to_broadcast([P, 2])).then_inc(consts_loaded, 16)
            act.dma_start(gb[:, :], gate_b.to_broadcast([P, 1])).then_inc(consts_loaded, 16)
            act.dma_start(gamma[:, :], ln_gamma.to_broadcast([P, D])).then_inc(consts_loaded, 16)
            act.dma_start(beta[:, :], ln_beta.to_broadcast([P, D])).then_inc(consts_loaded, 16)
            act.wait_ge(alpha_v, 2)
            nc.scalar.activation(alpha[:, 3:4], alpha[:, 2:3], ACT.Exp, scale=-1.0).then_inc(alpha_a, 1)
            act.wait_ge(alpha_a, 1)
            nc.scalar.activation(alpha[:, 4:5], alpha[:, 3:4], ACT.Ln, bias=1.0).then_inc(alpha_a, 1)
            act.wait_ge(alpha_v, 5)
            act.wait_ge(consts_built, 8)

            def exp_age(k):
                wait(act, users_loaded, k.times(48, 48))
                wait(act, logs_summed, k.times(1))
                nc.scalar.activation(decay[:, :], age_n[:, :], ACT.Exp, scale=alpha[:, 7:8]).then_inc(age_exp_ready, 1)

            def log_decay(k):
                wait(act, decay_ready, k.times(1, 1))
                nc.scalar.activation(decay[:, :], decay[:, :], ACT.Ln, bias=tiny[:, 0:1]).then_inc(log_ready, 1)

            def exp_gate(k):
                wait(act, gate_chain, k.times(5, 5))
                nc.scalar.activation(ez, abs_z, ACT.Exp, scale=-1.0).then_inc(gate_exp, 1)

            def sum_products(g, c, first, end):
                if first == 0:
                    wait(act, products_ready, g.times(CHUNKS, c + 1))
                for j in range(first, end):
                    ins = nc.scalar.activation(products[c % 2][:, j, :], products[c % 2][:, j, :], ACT.Copy,
                                               accum_out=raw[g.const % 2][:, c, SV + j:SV + j + 1])
                if end == SP_:
                    ins.then_inc(scored_a, 1)

            def exponentials(g):
                wait(act, shifted, g.times(1, 1))
                wait(act, exp_sums_ready, g.times(1))
                wait(act, attn_w_ready, g.times(1))
                nc.scalar.activation(exps[:, :, :], logits[:, :, :], ACT.Exp).then_inc(exps_ready, 1)

            def copy_attended(g):
                wait(act, inv_den_ready, g.times(1, 1))
                wait(act, attended_turned, g.times(1))
                for h in range(2):
                    ins = nc.scalar.activation(attended[:, h, :], attn_ps[:, (D + 1) * h:(D + 1) * h + D], ACT.Copy,
                                               scale=inv_den[:, h:h + 1])
                ins.then_inc(attended_ready, 1)

            def copy_attended_t(k):
                wait(act, attended_turned, k.times(2, 2))
                wait(act, long_ready, k.times(1))
                nc.scalar.activation(attended_t[:, :], attended_t_ps, ACT.Copy).then_inc(attended_copied, 1)

            def copy_sums(g, h):
                wait(act, sums_ready, g.times(2, h + 1))
                wait(act, mean_turned, g.times(2, h))
                nc.scalar.activation(sums_sb[:, :], sums_ps[h][:, 0:D], ACT.Copy).then_inc(sums_copied, 1)

            def copy_mean(g, h):
                wait(act, mean_turned, g.times(2, h + 1))
                wait(act, query_ready, g.times(2, h))
                nc.scalar.activation(mean_t[:, :, :], mean_t_ps.rearrange("p (b t) -> p b t", t=1)
                                     .to_broadcast([P, PAIR * USERS_PER_CHUNK, BLOCKS]), ACT.Copy)\
                    .then_inc(mean_copied, 1)

            def copy_query(g, h):
                wait(act, products_ready, g.times(CHUNKS, PAIR * (h + 1) - CHUNKS))
                wait(act, query_ready, g.times(2, h + 1))
                nc.scalar.activation(query_sb[h][:, :, :].rearrange("p c d -> p (c d)"), query_ps[h][:, 0:PAIR * D],
                                     ACT.Copy).then_inc(query_copied, 1)

            def inverse_deviation(k):
                wait(act, stats_ready, k.times(2, 2))
                nc.scalar.activation(ln_var, mean_var1, ACT.Ln, bias=tiny[:, 1:2]).then_inc(ln_var_ready, 1)
                wait(act, ln_var_ready, k.times(1, 1))
                nc.scalar.activation(rstd, ln_var, ACT.Exp, scale=-0.5).then_inc(rstd_ready, 1)

            def store(k):
                wait(act, result_ready, k.times(1, 1))
                act.dma_start(out_t[k.times(1)], result[:, :]).then_inc(stored, 16)

            def step(i):
                even, odd = i.const % 2 == 0, i.const % 2 == 1
                load, behind = i.inside(0, GROUPS), (i - 1).inside(0, GROUPS)
                gates, kg = odd and i.inside(-1, GROUPS - 1), (i + 1).per(2)
                prepare, kp = odd and i.inside(-3, GROUPS - 3), (i + 3).per(2)
                finish, kf = odd and i.inside(5, GROUPS + 5), (i - 5).per(2)
                if even and i.inside(6, GROUPS + 6):
                    store((i - 6).per(2))
                if (i - 3).inside(0, GROUPS):
                    copy_attended(i - 3)
                if behind:
                    sum_products(i - 1, 2, 0, 4)
                if load:
                    copy_sums(i, 0)
                if behind:
                    sum_products(i - 1, 2, 4, 9)
                if load:
                    copy_mean(i, 0)
                if behind:
                    sum_products(i - 1, 2, 9, SP_)
                if load:
                    copy_query(i, 0)
                if even and i.inside(4, GROUPS + 4):
                    copy_attended_t((i - 4).per(2))
                if behind:
                    sum_products(i - 1, 3, 0, SP_)
                if prepare:
                    exp_age(kp)
                if gates:
                    exp_gate(kg)
                if load:
                    copy_sums(i, 1)
                    sum_products(i, 0, 0, 6)
                    copy_mean(i, 1)
                    sum_products(i, 0, 6, SP_)
                if prepare:
                    log_decay(kp)
                if finish:
                    inverse_deviation(kf)
                if load:
                    sum_products(i, 1, 0, 5)
                if behind:
                    exponentials(i - 1)
                if load:
                    copy_query(i, 1)
                    sum_products(i, 1, 5, SP_)

            run_steps(act, step, -3, GROUPS + 4)
            act.wait_ge(stored, 16 * TILES)

        @block.tensor
        def _(pe):
            pe.wait_ge(consts_loaded, 16 * 8)
            pe.wait_ge(consts_built, 13)
            pe.matmul(max_ps[:, 0:D], wq_sb, wk_sb, start=True, stop=True).then_inc(weights_ps, 1)
            pe.transpose(val_ps[:, 0:D], wv_sb, ident[:, :]).then_inc(weights_ps, 1)
            pe.wait_ge(weights_ready, 2)
            pe.wait_ge(psum_cleared, 4)

            def masked_sums(g, h, q):
                if q == 0:
                    wait(pe, mask_w_ready, g.times(1, 1))
                    wait(pe, sums_copied, g.times(2, h - 1))
                pe.wait_ge(x_loaded[g.const % X_SLOTS][HALVES * h + q], g.per(X_SLOTS).times(16, 16))
                first, end = HALF[q], HALF[q + 1]
                for j in range(first, end):
                    for c in range(PAIR):
                        at = STRIP * (2 * c + j % 2)
                        mm = pe.matmul(sums_ps[h][at:at + USERS_PER_CHUNK, 0:D],
                                       mask_w[g.const % 2][:, PAIR * h + c, j, :],
                                       x[g.const % X_SLOTS][:, PAIR * h + c, j, :], start=(j < 2), stop=(j >= J - 2))
                if q == HALVES - 1:
                    mm.then_inc(sums_ready, 1)

            def turn_sums(g, h):
                wait(pe, sums_copied, g.times(2, h + 1))
                pe.matmul(mean_t_ps, sums_sb[:, :], pick[:, :, :].rearrange("p c b -> p (c b)"),
                          start=True, stop=True).then_inc(mean_turned, 1)

            def queries(g, h):
                wait(pe, mean_copied, g.times(2, h + 1))
                wait(pe, scored_v, g.times(2 * CHUNKS, 2 * (PAIR * (h + 1) - CHUNKS)))
                for c in range(PAIR):
                    users = mean_t[:, USERS_PER_CHUNK * c:USERS_PER_CHUNK * (c + 1), :]
                    mm = pe.matmul(query_ps[h][:, D * c:D * (c + 1)], users.rearrange("p b t -> p (b t)"),
                                   qk[:, :], start=True, stop=True)
                mm.then_inc(query_ready, 1)

            def turn_maxes(g):
                wait(pe, maxes_ready, g.times(1, 1))
                pe.transpose(max_t_ps, maxes[:, :], ident[:, :]).then_inc(maxes_turned, 1)

            def spread_gmax(g):
                wait(pe, gmax_ready, g.times(2, 2))
                pe.matmul(max_p_ps, gmax_wide[:, :, :].rearrange("c b t -> c (b t)"),
                          ident[0:CHUNKS, 0:CHUNKS], start=True, stop=True).then_inc(gmax_spread, 1)

            def attention_sums(g, h, first, end):
                if h == 0 and first == 0:
                    wait(pe, attn_w_ready, g.times(1, 1))
                    wait(pe, attended_ready, g.times(1))
                at_h = (D + 1) * h
                for j in range(first, end):
                    for c in range(PAIR):
                        at = STRIP * (2 * c + j % 2)
                        mm = pe.matmul(attn_ps[at:at + USERS_PER_CHUNK, at_h:at_h + D],
                                       attn_w[:, PAIR * h + c, j, :], x[g.const % X_SLOTS][:, PAIR * h + c, j, :],
                                       start=(j < 2), stop=(j >= J - 2))
                if end == J:
                    mm.then_inc(x_free, 1)

            def softmax_denominators(g):
                wait(pe, exp_sums_ready, g.times(1, 1))
                for h in range(2):
                    for c in range(PAIR):
                        for at in (2 * STRIP * c, 2 * STRIP * c + STRIP):
                            mm = pe.matmul(attn_ps[at:at + USERS_PER_CHUNK, (D + 1) * h + D:(D + 1) * (h + 1)],
                                           own[:, :], exp_sums[:, PAIR * h + c:PAIR * h + c + 1],
                                           start=True, stop=True)
                mm.then_inc(attn_sums_ready, 1)

            def turn_attended(g):
                wait(pe, attended_ready, g.times(1, 1))
                wait(pe, attended_copied, g.per(2).times(1))
                for h in range(2):
                    at = GROUP * (g.const % 2) + PAIR * USERS_PER_CHUNK * h
                    mm = pe.matmul(attended_t_ps[:, at:at + PAIR * USERS_PER_CHUNK], attended[:, h, :],
                                   pick[:, :, :].rearrange("p c b -> p (c b)"), start=True, stop=True)
                mm.then_inc(attended_turned, 1)

            def project_values(k):
                wait(pe, attended_copied, k.times(1, 1))
                wait(pe, shifted, k.times(2, 4 if (k + 1).inside(0, TILES) else 2))
                pe.matmul(long_ps, attended_t[:, :], wv_t[:, :], start=True, stop=True).then_inc(long_ready, 1)

            def step(i):
                load, attend, g = i.inside(0, GROUPS), (i - 2).inside(0, GROUPS), i - 2
                if i.const % 2 == 1 and i.inside(5, GROUPS + 5):
                    project_values((i - 5).per(2))
                if load:
                    masked_sums(i, 0, 0)
                    masked_sums(i, 0, 1)
                if attend:
                    attention_sums(g, 0, 0, 8)
                if load:
                    turn_sums(i, 0)
                if attend:
                    attention_sums(g, 0, 8, J)
                if load:
                    queries(i, 0)
                if (i - 3).inside(0, GROUPS):
                    turn_attended(i - 3)
                if load:
                    masked_sums(i, 1, 0)
                    masked_sums(i, 1, 1)
                if attend:
                    attention_sums(g, 1, 0, 8)
                if load:
                    turn_sums(i, 1)
                if attend:
                    attention_sums(g, 1, 8, 16)
                if (i - 1).inside(0, GROUPS):
                    turn_maxes(i - 1)
                if attend:
                    attention_sums(g, 1, 16, J)
                    softmax_denominators(g)
                if load:
                    queries(i, 1)
                if (i - 1).inside(0, GROUPS):
                    spread_gmax(i - 1)

            run_steps(pe, step, 0, GROUPS + 3)

        @block.vector
        def _(dve):
            for bank in (sums_ps[0], sums_ps[1], attn_ps):
                nc.vector.memset(bank[:, :], 0.0).then_inc(psum_cleared, 1)
            dve.wait_ge(psum_cleared, 3)
            nc.vector.memset(dens_ps, 1.0).then_inc(psum_cleared, 1)
            dve.wait_ge(consts_built, 8)
            nc.vector.tensor_copy(times[:, :], times_i).then_inc(consts_cast, 1)
            nc.vector.tensor_copy(row_base[:, :], base_i[:, :]).then_inc(consts_cast, 1)
            dve.wait_ge(consts_loaded, 16 * 8)
            nc.vector.tensor_scalar(alpha[:, 1:2], alpha[:, 0:1], -1.0, None, ALU.mult).then_inc(alpha_v, 1)
            dve.wait_ge(alpha_v, 1)
            nc.vector.tensor_tensor(alpha[:, 2:3], alpha[:, 0:1], alpha[:, 1:2], ALU.max).then_inc(alpha_v, 1)
            nc.vector.tensor_scalar(alpha[:, 5:6], alpha[:, 0:1], 0.0, None, ALU.max).then_inc(alpha_v, 1)
            dve.wait_ge(alpha_v, 3)
            dve.wait_ge(alpha_a, 2)
            nc.vector.tensor_tensor(alpha[:, 6:7], alpha[:, 5:6], alpha[:, 4:5], ALU.add).then_inc(alpha_v, 1)
            dve.wait_ge(alpha_v, 4)
            nc.vector.tensor_scalar(alpha[:, 7:8], alpha[:, 6:7], 1e-6, -1.0, ALU.add, ALU.mult).then_inc(alpha_v, 1)
            dve.wait_ge(weights_ps, 2)
            nc.vector.tensor_copy(qk[:, :], max_ps[:, 0:D]).then_inc(weights_ready, 1)
            nc.vector.tensor_copy(wv_t[:, :], val_ps[:, 0:D]).then_inc(weights_ready, 1)
            dve.wait_ge(consts_cast, 2)

            def build_mask_weights(g):
                k = g.per(2)
                wait(dve, logs_spread[k.const % TILE_RING], spread_count(k))
                wait(dve, sums_ready, g.times(2, -2))
                logs = logs_p[g.const % UNROLL]
                for c in range(CHUNKS):
                    w = nc.vector.scalar_tensor_tensor(
                        out=mask_w[g.const % 2][:, c, :, :],
                        in0=logs[:, c, 0:J].rearrange("p (j b) -> p j b", b=1).to_broadcast([P, J, USERS_PER_CHUNK]),
                        scalar=MASKED / 2,
                        in1=own[:, :].rearrange("p (j b) -> p j b", j=1).to_broadcast([P, J, USERS_PER_CHUNK]),
                        op0=ALU.is_gt, op1=ALU.mult)
                w.then_inc(mask_w_ready, 1)

            def score(g, c, first, end):
                h = c // PAIR
                if first == 0 and c % PAIR == 0:
                    wait(dve, query_copied, g.times(2, h + 1))
                for j in range(first, end):
                    if j in (0, SV_HALF):
                        wait(dve, scored_v, g.times(2 * CHUNKS, 2 * c - 1 + (j > 0)))
                    ins = nc.vector.tensor_tensor_reduce(
                        unused_v[:, j, :], x[g.const % X_SLOTS][:, c, j, :], query_ps[h][:, D * (c % PAIR):D * (c % PAIR + 1)],
                        1.0, 0.0, ALU.mult, ALU.add, raw[g.const % 2][:, c, j:j + 1])
                    if j in (SV_HALF - 1, SV - 1):
                        ins.then_inc(scored_v, 1)

            def scale_logits(g):
                wait(dve, scored_a, g.times(CHUNKS, CHUNKS))
                wait(dve, scored_v, g.times(2 * CHUNKS, 2 * CHUNKS))
                wait(dve, exps_ready, g.times(1))
                logs = logs_p[g.const % UNROLL]
                nc.vector.tensor_tensor(logits[:, :, :], raw[g.const % 2][:, :, :],
                                        logs[:, :, J:J + 1].to_broadcast([P, CHUNKS, J]), ALU.mult)\
                    .then_inc(logits_scaled, 1)

            def add_logs(g):
                wait(dve, logits_scaled, g.times(1, 1))
                nc.vector.tensor_tensor(logits[:, :, :], logits[:, :, :], logs_p[g.const % UNROLL][:, :, 0:J], ALU.add)\
                    .then_inc(logits_ready, 1)

            def partition_maxes(g):
                wait(dve, logits_ready, g.times(1, 1))
                nc.vector.tensor_reduce(maxes[:, :], logits[:, :, :], AX_X, ALU.max).then_inc(maxes_ready, 1)

            def user_maxes(g):
                wait(dve, maxes_turned, g.times(1, 1))
                nc.vector.tensor_reduce(gmax[:, :], max_t_ps.rearrange("c (b t) -> c b t", t=BLOCKS), AX_X, ALU.max)\
                    .then_inc(gmax_ready, 1)

            def widen_maxes(g):
                wait(dve, gmax_ready, g.times(2, 1))
                nc.vector.tensor_copy(gmax_wide[:, :, :], gmax[:, :].rearrange("c (b t) -> c b t", t=1)
                                      .to_broadcast([CHUNKS, USERS_PER_CHUNK, BLOCKS])).then_inc(gmax_ready, 1)

            def shift(g):
                wait(dve, gmax_spread, g.times(1, 1))
                nc.vector.tensor_tensor(logits[:, :, :], logits[:, :, :],
                                        max_p_ps.rearrange("p (c j) -> p c j", j=1).to_broadcast([P, CHUNKS, J]),
                                        ALU.subtract).then_inc(shifted, 1)

            def build_attention_weights(g):
                wait(dve, exps_ready, g.times(1, 1))
                wait(dve, x_free, g.times(2))
                nc.vector.tensor_tensor(
                    attn_w[:, :, :, :].rearrange("p c j b -> p (c j) b"),
                    exps[:, :, :].rearrange("p c (j b) -> p (c j) b", b=1).to_broadcast([P, CHUNKS * J, USERS_PER_CHUNK]),
                    own[:, :].rearrange("p (j b) -> p j b", j=1).to_broadcast([P, CHUNKS * J, USERS_PER_CHUNK]),
                    ALU.mult).then_inc(attn_w_ready, 1)
                wait(dve, attn_sums_ready, g.times(1))
                nc.vector.tensor_reduce(exp_sums[:, :], exps[:, :, :], AX_X, ALU.add).then_inc(exp_sums_ready, 1)

            def invert_denominators(g):
                wait(dve, attn_sums_ready, g.times(1, 1))
                wait(dve, attended_ready, g.times(1))
                nc.vector.reciprocal(inv_den[:, :], dens_ps).then_inc(inv_den_ready, 1)

            def count_masks(k):
                wait(dve, users_loaded, k.times(48, 48))
                wait(dve, decay_ready, k.times(1))
                wait(dve, penalty_ready, k.times(1))
                nc.vector.tensor_scalar(maskf[:, :], mask_n[:, :], 1.0, None, ALU.mult, ALU.add, accum_out=cnt)\
                    .then_inc(maskf_ready, 1)

            def bound_counts(k):
                wait(dve, maskf_ready, k.times(1, 1))
                nc.vector.tensor_scalar(cnt1, cnt, 1.0, None, ALU.max).then_inc(user_counts, 1)
                nc.vector.tensor_scalar(cnt_eps, cnt, 1e-6, None, ALU.add).then_inc(user_counts, 1)
                nc.vector.tensor_scalar(cnt_min, cnt, 1.0, None, ALU.min).then_inc(user_counts, 1)

            def invert_counts(k):
                wait(dve, user_counts, k.times(3, 3))
                nc.vector.tensor_scalar(denom, cnt1, float(WINDOW), None, ALU.min).then_inc(user_derived, 1)
                nc.vector.reciprocal(inv_eps, cnt_eps).then_inc(user_derived, 1)
                nc.vector.reciprocal(inv_min, cnt_min).then_inc(user_derived, 1)
                nc.vector.tensor_scalar(below[:, :], times[:, :], cnt1, None, ALU.is_lt).then_inc(user_windows, 1)

            def place_windows(k):
                wait(dve, user_derived, k.times(3, 3))
                nc.vector.tensor_tensor(start, cnt1, denom, ALU.subtract).then_inc(user_windows, 1)
                nc.vector.reciprocal(inv_denom, denom).then_inc(user_windows, 1)
                kk = k - 1
                if kk.inside(0, TILES):
                    wait(dve, logs_spread[kk.const % TILE_RING], spread_count(kk))
                nc.vector.tensor_scalar(logs_n[:, :, J], ones8[:, :], inv_eps, SCALE, ALU.mult, ALU.mult)\
                    .then_inc(scale_ready, 1)

            def window_weights(k):
                wait(dve, user_windows, k.times(4, 3))
                wait(dve, row_base_moved, k.times(1))
                wait(dve, window_loaded, k.times(16 * WINDOW, 16 * WINDOW * (1 - TILE_RING)))
                nc.vector.tensor_tensor(row_idx[k.const % TILE_RING][:, :], start, row_base[:, :], ALU.add)\
                    .then_inc(row_idx_ready, 1)
                nc.vector.tensor_scalar(win_w[:, :], times[:, 0:WINDOW], denom, inv_denom, ALU.is_lt, ALU.mult)\
                    .then_inc(user_windows, 1)
                nc.vector.scalar_tensor_tensor(out=below[:, :], in0=times[:, :], scalar=start, in1=below[:, :],
                                               op0=ALU.is_ge, op1=ALU.mult).then_inc(lastk_ready, 1)

            def window_sums(k):
                wait(dve, row_idx_ready, k.times(1, 1))
                nc.vector.tensor_scalar(row_base[:, :], row_base[:, :], float(P * T), None, ALU.add)\
                    .then_inc(row_base_moved, 1)
                wait(dve, lastk_ready, k.times(1, 1))
                nc.vector.tensor_tensor_reduce(pop_n[:, :], pop_n[:, :], below[:, :], 1.0, 0.0, ALU.mult, ALU.add,
                                               pop_sum).then_inc(ctx_sums, 1)
                wait(dve, age_exp_ready, k.times(1, 1))
                nc.vector.tensor_tensor_reduce(age_n[:, :], age_n[:, :], below[:, :], 1.0, 0.0, ALU.mult, ALU.add,
                                               age_sum).then_inc(ctx_sums, 1)

            def gate_logit_pop(k):
                wait(dve, ctx_sums, k.times(2, 2))
                nc.vector.tensor_scalar(z1, pop_sum, gw[:, 0:1], None, ALU.mult).then_inc(gate_chain, 1)

            def gate_logit_age(k):
                wait(dve, gate_chain, k.times(5, 1))
                nc.vector.scalar_tensor_tensor(out=z2, in0=age_sum, scalar=gw[:, 1:2], in1=z1, op0=ALU.mult,
                                               op1=ALU.add).then_inc(gate_chain, 1)

            def gate_logit(k):
                wait(dve, gate_chain, k.times(5, 2))
                nc.vector.tensor_scalar(z, z2, inv_denom, gb[:, 0:1], ALU.mult, ALU.add).then_inc(gate_chain, 1)

            def gate_magnitude(k):
                wait(dve, gate_chain, k.times(5, 3))
                nc.vector.scalar_tensor_tensor(out=abs_z, in0=z, scalar=-1.0, in1=z, op0=ALU.mult, op1=ALU.max)\
                    .then_inc(gate_chain, 1)
                nc.vector.tensor_scalar(positive, z, 0.0, None, ALU.is_ge).then_inc(gate_chain, 1)

            def gate_denominator(k):
                wait(dve, gate_exp, k.times(1, 1))
                nc.vector.tensor_scalar(e1, ez, 1.0, None, ALU.add).then_inc(gate_tail, 1)

            def gate_large(k):
                wait(dve, gate_tail, k.times(6, 1))
                nc.vector.reciprocal(large, e1).then_inc(gate_tail, 1)

            def gate_small(k):
                wait(dve, gate_tail, k.times(6, 2))
                nc.vector.tensor_tensor(small, ez, large, ALU.mult).then_inc(gate_tail, 1)

            def gate_gap(k):
                wait(dve, gate_tail, k.times(6, 3))
                nc.vector.tensor_tensor(gap, large, small, ALU.subtract).then_inc(gate_tail, 1)

            def gate_value(k):
                wait(dve, gate_tail, k.times(6, 4))
                nc.vector.scalar_tensor_tensor(out=gate, in0=gap, scalar=positive, in1=small, op0=ALU.mult,
                                               op1=ALU.add).then_inc(gate_tail, 1)

            def gate_rest(k):
                wait(dve, gate_tail, k.times(6, 5))
                nc.vector.tensor_scalar(omg, gate, -1.0, 1.0, ALU.mult, ALU.add).then_inc(gate_tail, 1)

            def gate_weights(k):
                wait(dve, user_windows, k.times(4, 4))
                nc.vector.tensor_scalar(gate_win[k.const % TILE_RING][:, :], win_w[:, :], gate, None, ALU.mult)\
                    .then_inc(gates_ready, 1)
                wait(dve, gate_tail, k.times(6, 6))
                nc.vector.tensor_tensor(gate_long[k.const % TILE_RING][:, :], omg, inv_min, ALU.mult)\
                    .then_inc(gates_ready, 1)

            def short_term(k, w):
                if w == 0:
                    wait(dve, window_loaded, k.times(16 * WINDOW, 16 * WINDOW))
                    wait(dve, gates_ready, k.times(2, 2))
                    nc.vector.tensor_scalar(user[:, :], window[:, 0, :], gate_win[k.const % TILE_RING][:, 0:1], None,
                                            ALU.mult).then_inc(short_sums, 1)
                else:
                    wait(dve, short_sums, k.times(WINDOW + 1, w))
                    nc.vector.scalar_tensor_tensor(out=user[:, :], in0=window[:, w, :],
                                                   scalar=gate_win[k.const % TILE_RING][:, w:w + 1], in1=user[:, :],
                                                   op0=ALU.mult, op1=ALU.add).then_inc(short_sums, 1)

            def add_long_term(k):
                wait(dve, long_ready, k.times(1, 1))
                wait(dve, short_sums, k.times(WINDOW + 1, WINDOW))
                nc.vector.scalar_tensor_tensor(out=user[:, :], in0=long_ps, scalar=gate_long[k.const % TILE_RING][:, 0:1],
                                               in1=user[:, :], op0=ALU.mult, op1=ALU.add).then_inc(short_sums, 1)

            def measure(k):
                wait(dve, short_sums, k.times(WINDOW + 1, WINDOW + 1))
                nc.vector.bn_stats(stats[:, :], user[:, :]).then_inc(stats_ready, 1)

            def measure_all(k):
                hold(dve, stats_ready, k.times(2, 1), held["vector"])
                nc.vector.bn_aggr(mean_var, stats[:, :]).then_inc(stats_ready, 1)

            def normalise(k):
                wait(dve, rstd_ready, k.times(1, 1))
                wait(dve, stored, k.times(16))
                nc.vector.tensor_scalar(result[:, :], user[:, :], mean_var0, rstd, ALU.subtract, ALU.mult)\
                    .then_inc(normed_ready, 1)

            def scale_normed(k):
                wait(dve, normed_ready, k.times(2, 1))
                nc.vector.tensor_tensor(result[:, :], result[:, :], gamma[:, :], ALU.mult).then_inc(normed_ready, 1)

            def add_beta(k):
                wait(dve, normed_ready, k.times(2, 2))
                nc.vector.tensor_tensor(result[:, :], result[:, :], beta[:, :], ALU.add).then_inc(result_ready, 1)

            def step(i):
                g, d, odd = i - 1, i - 1, i.const % 2 == 1
                behind, ahead = g.inside(0, GROUPS), i.inside(0, GROUPS)
                logs, kl = not odd and i.inside(-2, GROUPS - 2), (i + 2).per(2)
                gates, kg = odd and i.inside(-1, GROUPS - 1), (i + 1).per(2)
                finish, kf = odd and i.inside(5, GROUPS + 5), (i - 5).per(2)

                def part(c, first, end):
                    if c >= PAIR and behind:
                        score(g, c, first, end)
                    if c < PAIR and ahead:
                        score(i, c, first, end)

                if (i - 3).inside(0, GROUPS):
                    invert_denominators(i - 3)
                part(2, 0, 2)
                if logs:
                    bound_counts(kl)
                if gates:
                    window_weights(kg)
                part(2, 2, 5)
                if gates:
                    window_sums(kg)
                if logs:
                    invert_counts(kl)
                if finish:
                    short_term(kf, 0)
                part(2, 5, 8)
                if logs:
                    place_windows(kl)
                if finish:
                    short_term(kf, 1)
                part(2, 8, 11)
                if finish:
                    short_term(kf, 2)
                part(2, 11, SV)
                part(3, 0, 2)
                if finish:
                    short_term(kf, 3)
                part(3, 2, 5)
                if gates:
                    gate_logit_pop(kg)
                if finish:
                    short_term(kf, 4)
                part(3, 5, 8)
                if gates:
                    gate_logit_age(kg)
                if finish:
                    add_long_term(kf)
                part(3, 8, 11)
                if gates:
                    gate_logit(kg)
                if finish:
                    measure(kf)
                part(3, 11, SV)
                if gates:
                    gate_magnitude(kg)
                if finish:
                    measure_all(kf)
                if odd and i.inside(-3, GROUPS - 3):
                    count_masks((i + 3).per(2))
                part(0, 0, 2)
                if (i + 1).inside(0, GROUPS):
                    build_mask_weights(i + 1)
                part(0, 2, 5)
                if behind:
                    scale_logits(d)
                part(0, 5, 7)
                if behind:
                    add_logs(d)
                part(0, 7, 9)
                if behind:
                    partition_maxes(d)
                if finish:
                    normalise(kf)
                part(0, 9, SV)
                if behind:
                    user_maxes(d)
                if finish:
                    scale_normed(kf)
                if gates:
                    gate_denominator(kg)
                part(1, 0, 2)
                if behind:
                    widen_maxes(d)
                if finish:
                    add_beta(kf)
                if gates:
                    gate_large(kg)
                part(1, 2, 5)
                if behind:
                    shift(d)
                if gates:
                    gate_small(kg)
                part(1, 5, 7)
                if gates:
                    gate_gap(kg)
                part(1, 7, 9)
                if gates:
                    gate_value(kg)
                part(1, 9, 11)
                if gates:
                    gate_rest(kg)
                if behind:
                    build_attention_weights(d)
                if gates:
                    gate_weights(kg)
                part(1, 11, SV)

            run_steps(dve, step, -3, GROUPS + 3)


_INS = ["r_hist_items", "r_hist_mask", "r_hist_age_hours", "r_hist_popularity", "L0_rec_Wq", "L0_rec_Wk",
        "L0_rec_Wv", "L0_rec_gate_w", "L0_rec_gate_b", "L0_rec_ln_gamma", "L0_rec_ln_beta", "L0_rec_decay_alpha"]


def kernel(**inputs):
    import numpy as np
    import concourse.bacc as bacc
    from concourse.bass_utils import run_bass_kernel_spmd

    nc = bacc.Bacc("TRN2", target_bir_lowering=False, num_devices=1)
    arrays, args = {}, []
    for name in _INS:
        a = np.ascontiguousarray(inputs[name])
        if a.ndim < 2:
            a = a.reshape(1, -1)
        arrays[f"in_{name}_dram"] = a
        args.append(nc.dram_tensor(f"in_{name}_dram", a.shape, mybir.dt.from_np(a.dtype), kind="ExternalInput").ap())
    users, _, dims = inputs["r_hist_items"].shape
    out = nc.dram_tensor("out_0_dram", (users, dims), F32, kind="ExternalOutput").ap()
    build(nc, *args, out)
    r = run_bass_kernel_spmd(nc, [arrays], core_ids=[0])
    return r.results[0]["out_0_dram"]
```

```python
from contextlib import ExitStack

import concourse.bass as bass
from concourse import mybir

F32 = mybir.dt.float32
BF16 = mybir.dt.bfloat16
I32 = mybir.dt.int32
U8 = mybir.dt.uint8
ALU = mybir.AluOpType
ACT = mybir.ActivationFunctionType
AX_X = mybir.AxisListType.X

P = 128
USERS_PER_CHUNK = 16
CHUNKS = 4
PAIR = 2
STRIP = P // (2 * PAIR)
GROUP = USERS_PER_CHUNK * CHUNKS
BLOCKS = P // USERS_PER_CHUNK
WINDOW = 5
X_SLOTS = 3
UNROLL = 6
TILE_RING = UNROLL // 2
FIRST_LOOP, LOOPS = 5, 4
MASKED = -1.0e30
HALVES = 2
SV = 13

SV_HALF = (SV + 1) // 2


class Step:

    def __init__(self, const, it=None, stride=UNROLL):
        self.const, self.it, self.stride = const, it, stride

    def __add__(self, n):
        return Step(self.const + n, self.it, self.stride)

    def __sub__(self, n):
        return self + -n

    def per(self, n):
        return Step(self.const // n, self.it, self.stride // n)

    def times(self, factor, plus=0):
        if self.it is None:
            return factor * self.const + plus
        return self.it * (factor * self.stride) + (factor * self.const + plus)

    def due(self, factor, plus=0):
        return self.it is not None or factor * self.const + plus > 0

    def inside(self, first, end):
        return self.it is not None or first <= self.const < end


def run_steps(eng, step, first, last):
    for i in range(first, FIRST_LOOP):
        step(Step(i))
    with eng.Fori(0, LOOPS) as it:
        for u in range(UNROLL):
            step(Step(FIRST_LOOP + u, it))
    for i in range(FIRST_LOOP + UNROLL * LOOPS, last + 1):
        step(Step(i))


def build(nc, items, mask, age, popularity, Wq, Wk, Wv, gate_w, gate_b, ln_gamma, ln_beta, decay_alpha, out):
    USERS, T, D = items.shape
    J = T // BLOCKS
    HALF = [0, (J + 1) // 2, J]
    GROUPS = USERS // GROUP
    TILES = USERS // P
    SP_ = J - SV
    SCALE = 1.0 / float(D) ** 0.5
    assert D == P and GROUPS >= FIRST_LOOP + UNROLL * LOOPS

    items_g = items.rearrange("(g c b) (t j) d -> g (b t) c (j d)", c=CHUNKS, b=USERS_PER_CHUNK, t=BLOCKS)
    rows = items.rearrange("u t d -> (u t) d")
    age_t = age.rearrange("(k p) t -> k p t", p=P)
    pop_t = popularity.rearrange("(k p) t -> k p t", p=P)
    mask_t = mask.rearrange("(k p) t -> k p t", p=P)
    out_t = out.rearrange("(k p) d -> k p d", p=P)

    ctx = ExitStack()
    with ctx:
        def sb(name, shape, dt=F32):
            return ctx.enter_context(nc.sbuf_tensor(name, shape, dt))

        def ps(name):
            return ctx.enter_context(nc.psum_tensor(name, [P, 512], F32))

        def sem(name):
            return ctx.enter_context(nc.semaphore(name))

        x = [sb(f"x{s}", [P, CHUNKS, J, D]) for s in range(X_SLOTS)]
        products = [sb(f"products{s}", [P, SP_, D]) for s in range(2)]
        mask_w = [sb(f"mask_w{s}", [P, CHUNKS, J, USERS_PER_CHUNK]) for s in range(2)]
        attn_w = sb("attn_w", [P, CHUNKS, J, USERS_PER_CHUNK])
        query_sb = [sb(f"query_sb{h}", [P, PAIR, D]) for h in range(2)]
        unused_v = sb("unused_v", [P, SV, D], BF16)
        logs_p = [sb(f"logs_p{s}", [P, CHUNKS, J + 1]) for s in range(UNROLL)]
        raw = [sb(f"raw{s}", [P, CHUNKS, J]) for s in range(2)]
        logits = sb("logits", [P, CHUNKS, J])
        exps = sb("exps", [P, CHUNKS, J])
        maxes = sb("maxes", [P, CHUNKS])
        gmax = sb("gmax", [CHUNKS, USERS_PER_CHUNK])
        gmax_wide = sb("gmax_wide", [CHUNKS, USERS_PER_CHUNK, BLOCKS])
        exp_sums = sb("exp_sums", [P, CHUNKS])
        sums_sb = sb("sums_sb", [P, D])
        mean_t = sb("mean_t", [P, PAIR * USERS_PER_CHUNK, BLOCKS])
        inv_den = sb("inv_den", [P, 2])
        attended = sb("attended", [P, 2, D])
        attended_t = sb("attended_t", [P, P])
        age_n = sb("age_n", [P, T])
        pop_n = sb("pop_n", [P, T])
        mask_n = sb("mask_n", [P, T], U8)
        maskf = sb("maskf", [P, T])
        decay = sb("decay", [P, T])
        logs_n = sb("logs_n", [P, BLOCKS, J + 1])
        below = sb("below", [P, T])
        u = sb("u", [P, 28])
        (cnt, cnt1, cnt_eps, cnt_min, denom, inv_eps, inv_min, start, inv_denom, pop_sum, age_sum, z1, z2, z, ez,
         e1, gate, omg, large, mean_var0, mean_var1, ln_var, rstd, abs_z, positive, small,
         gap) = [u[:, n:n + 1] for n in range(27)]
        mean_var = u[:, 19:21]
        row_base = sb("row_base", [P, 1])
        win_w = sb("win_w", [P, WINDOW])
        gate_win = [sb(f"gate_win{s}", [P, WINDOW]) for s in range(TILE_RING)]
        gate_long = [sb(f"gate_long{s}", [P, 1]) for s in range(TILE_RING)]
        row_idx = [sb(f"row_idx{s}", [P, 1], I32) for s in range(TILE_RING)]
        window = sb("window", [P, WINDOW, D])
        user = sb("user", [P, D])
        stats = sb("stats", [P, 6])
        result = sb("result", [P, D])
        ident = sb("ident", [P, P])
        own = sb("own", [P, USERS_PER_CHUNK])
        pick = sb("pick", [P, PAIR, USERS_PER_CHUNK])
        times_i = maskf[:, :].bitcast(I32)
        times = sb("times", [P, T])
        base_i = sb("base_i", [P, 1], I32)
        ones8 = sb("ones8", [P, BLOCKS])
        tiny = sb("tiny", [P, 2])
        qk = sb("qk", [P, D])
        wv_t = sb("wv_t", [P, D])
        gamma = sb("gamma", [P, D])
        beta = sb("beta", [P, D])
        gw = sb("gw", [P, 2])
        gb = sb("gb", [P, 1])
        alpha = sb("alpha", [P, 8])
        wq_sb, wk_sb, wv_sb = [products[0][:, n, :] for n in range(3)]

        sums_ps = [ps("sums_ps0"), ps("sums_ps1")]
        query_ps = [ps("query_ps0"), ps("query_ps1")]
        attn_ps = ps("attn_ps")
        turn_ps = ps("turn_ps")
        max_ps = ps("max_ps")
        val_ps = ps("val_ps")
        dens_ps = attn_ps[:, 0:PAIR * (D + 1)].rearrange("p (h w) -> p h w", h=PAIR)[:, :, D]
        mean_t_ps = turn_ps[:, 0:PAIR * USERS_PER_CHUNK]
        max_t_ps = max_ps[0:CHUNKS, 0:P]
        max_p_ps = max_ps[:, P:P + CHUNKS]
        attended_t_ps = val_ps[:, 0:P]
        long_ps = max_ps[:, P + CHUNKS:P + CHUNKS + D]

        x_loaded = [[sem(f"x_loaded{s}_{n}") for n in range(2 * HALVES)] for s in range(X_SLOTS)]
        x_free = sem("x_free")
        users_loaded = sem("users_loaded")
        weights_loaded = sem("weights_loaded")
        consts_loaded = sem("consts_loaded")
        alpha_loaded = sem("alpha_loaded")
        consts_built = sem("consts_built")
        consts_cast = sem("consts_cast")
        weights_ps = sem("weights_ps")
        weights_ready = sem("weights_ready")
        psum_cleared = sem("psum_cleared")
        alpha_v = sem("alpha_v")
        alpha_a = sem("alpha_a")

        mask_w_ready = sem("mask_w_ready")
        sums_ready = sem("sums_ready")
        sums_copied = sem("sums_copied")
        mean_turned = sem("mean_turned")
        mean_copied = sem("mean_copied")
        query_ready = sem("query_ready")
        query_copied = sem("query_copied")
        products_ready = sem("products_ready")
        scored_a = sem("scored_a")
        scored_v = sem("scored_v")
        logits_scaled = sem("logits_scaled")
        logits_ready = sem("logits_ready")
        maxes_ready = sem("maxes_ready")
        maxes_turned = sem("maxes_turned")
        gmax_ready = sem("gmax_ready")
        gmax_spread = sem("gmax_spread")
        shifted = sem("shifted")
        exps_ready = sem("exps_ready")
        attn_w_ready = sem("attn_w_ready")
        exp_sums_ready = sem("exp_sums_ready")
        attn_sums_ready = sem("attn_sums_ready")
        inv_den_ready = sem("inv_den_ready")
        attended_ready = sem("attended_ready")
        attended_turned = sem("attended_turned")
        attended_copied = sem("attended_copied")
        long_ready = sem("long_ready")

        maskf_ready = sem("maskf_ready")
        age_exp_ready = sem("age_exp_ready")
        decay_ready = sem("decay_ready")
        penalty_ready = sem("penalty_ready")
        log_ready = sem("log_ready")
        logs_summed = sem("logs_summed")
        scale_ready = sem("scale_ready")
        logs_spread = [[sem(f"logs_spread{s}_{h}") for h in range(2)] for s in range(TILE_RING)]
        user_counts = sem("user_counts")
        user_derived = sem("user_derived")
        scale_chain = sem("scale_chain")
        user_windows = sem("user_windows")
        row_idx_ready = sem("row_idx_ready")
        lastk_ready = sem("lastk_ready")
        ctx_sums = sem("ctx_sums")
        gate_chain = sem("gate_chain")
        gate_exp = sem("gate_exp")
        gate_tail = sem("gate_tail")
        gates_ready = sem("gates_ready")
        row_base_moved = sem("row_base_moved")
        window_loaded = sem("window_loaded")
        short_sums = sem("short_sums")
        stats_ready = sem("stats_ready")
        ln_var_ready = sem("ln_var_ready")
        rstd_ready = sem("rstd_ready")
        centred = sem("centred")
        result_ready = sem("result_ready")
        held_sync, held_gpsimd, held_vector = sem("held_sync"), sem("held_gpsimd"), sem("held_vector")
        stored = sem("stored")

        block = ctx.enter_context(nc.Block())

        def spread_count(k):
            return k.per(TILE_RING).times(16 * CHUNKS, 16 * CHUNKS)

        @block.sync
        def _(sp):
            def load_users(k):
                if k.due(2):
                    sp.wait_ge(ctx_sums, k.times(2))
                sp.sem_inc(held_sync, 1)
                if k.due(1):
                    sp.wait_ge(age_exp_ready, k.times(1))
                sp.sem_inc(held_sync, 1)
                at = k.times(1)
                sp.dma_start(mask_n[:, :], mask_t[at]).then_inc(users_loaded, 16)
                sp.dma_start(age_n[:, :], age_t[at]).then_inc(users_loaded, 16)
                sp.dma_start(pop_n[:, :], pop_t[at]).then_inc(users_loaded, 16)

            def load_rows(g, h):
                if g.due(2, h + 1 - 2 * X_SLOTS):
                    sp.wait_ge(x_free, g.times(2, h + 1 - 2 * X_SLOTS))
                sp.sem_inc(held_sync, 1)
                for q in range(HALVES):
                    sp.dma_start(x[g.const % X_SLOTS][:, PAIR * h:PAIR * (h + 1), HALF[q]:HALF[q + 1], :]
                                 .rearrange("p c j d -> p c (j d)"),
                                 items_g[g.times(1)][:, PAIR * h:PAIR * (h + 1), HALF[q] * D:HALF[q + 1] * D])\
                      .then_inc(x_loaded[g.const % X_SLOTS][HALVES * h + q], 16)

            def spread_logs(k, h):
                if h == 0:
                    sp.wait_ge(logs_summed, k.times(1, 1))
                    sp.sem_inc(held_sync, 1)
                    sp.wait_ge(scale_ready, k.times(1, 1))
                    sp.sem_inc(held_sync, 1)
                for c in range(CHUNKS):
                    first = (h * CHUNKS + c) * USERS_PER_CHUNK
                    sp.dma_start(logs_p[(2 * k.const + h) % UNROLL][:, c, :],
                                 logs_n[first:first + USERS_PER_CHUNK, :, :])\
                      .then_inc(logs_spread[k.const % TILE_RING][h], 16)

            def step(i):
                even, odd = i.const % 2 == 0, i.const % 2 == 1
                if odd and i.inside(1, GROUPS - 3):
                    load_users((i + 3).per(2))
                if even and i.inside(0, GROUPS - 2):
                    spread_logs((i + 2).per(2), 0)
                if i.inside(1, GROUPS - 1):
                    load_rows(i + 1, 0)
                if even and i.inside(0, GROUPS - 2):
                    spread_logs((i + 2).per(2), 1)
                if i.inside(1, GROUPS - 1):
                    load_rows(i + 1, 1)

            load_users(Step(0))
            load_rows(Step(0), 0)
            spread_logs(Step(0), 0)
            load_users(Step(1))
            load_rows(Step(0), 1)
            spread_logs(Step(0), 1)
            load_rows(Step(1), 0)
            load_rows(Step(1), 1)
            run_steps(sp, step, 0, GROUPS - 2)

        @block.gpsimd
        def _(pool):
            nc.gpsimd.memset(ident[:, :], 0.0).then_inc(consts_built, 1)
            nc.gpsimd.memset(pick[:, :, :], 0.0).then_inc(consts_built, 1)
            nc.gpsimd.memset(own[:, :], 1.0).then_inc(consts_built, 1)
            nc.gpsimd.memset(ones8[:, :], 1.0).then_inc(consts_built, 1)
            nc.gpsimd.memset(tiny[:, 0:1], 1e-12).then_inc(consts_built, 1)
            nc.gpsimd.memset(tiny[:, 1:2], 1e-5).then_inc(consts_built, 1)
            nc.gpsimd.iota(times_i, [[1, T]], base=0, channel_multiplier=0).then_inc(consts_built, 1)
            nc.gpsimd.iota(base_i[:, :], [[0, 1]], base=0, channel_multiplier=T).then_inc(consts_built, 1)
            pool.wait_ge(consts_built, 8)
            nc.gpsimd.affine_select(out=ident[:, :], in_=ident[:, :], compare_op=ALU.not_equal, fill=1.0, base=0,
                                    pattern=[[-1, P]], channel_multiplier=1).then_inc(consts_built, 1)
            nc.gpsimd.affine_select(out=own[:, :], in_=own[:, :], compare_op=ALU.is_ge, fill=0.0, base=0,
                                    pattern=[[-BLOCKS, USERS_PER_CHUNK]], channel_multiplier=1).then_inc(consts_built, 1)
            nc.gpsimd.affine_select(out=pick[:, :, :], in_=pick[:, :, :], compare_op=ALU.not_equal, fill=1.0, base=0,
                                    pattern=[[-2 * STRIP, PAIR], [-1, USERS_PER_CHUNK]], channel_multiplier=1)\
                .then_inc(consts_built, 1)
            pool.wait_ge(consts_built, 11)
            nc.gpsimd.affine_select(out=pick[:, :, :], in_=pick[:, :, :], compare_op=ALU.not_equal, fill=1.0,
                                    base=-STRIP, pattern=[[-2 * STRIP, PAIR], [-1, USERS_PER_CHUNK]],
                                    channel_multiplier=1).then_inc(consts_built, 1)
            nc.gpsimd.affine_select(out=own[:, :], in_=own[:, :], compare_op=ALU.is_ge, fill=0.0, base=BLOCKS - 1,
                                    pattern=[[BLOCKS, USERS_PER_CHUNK]], channel_multiplier=-1)\
                .then_inc(consts_built, 1)

            def multiply(g, c):
                pool.wait_ge(query_copied, g.times(2, c // PAIR + 1))
                if g.due(CHUNKS, c + 1 - 2):
                    pool.wait_ge(scored_a, g.times(CHUNKS, c + 1 - 2))
                nc.gpsimd.tensor_tensor(products[c % 2][:, :, :], x[g.const % X_SLOTS][:, c, SV:J, :],
                                        query_sb[c // PAIR][:, c % PAIR:c % PAIR + 1, :].to_broadcast([P, SP_, D]),
                                        ALU.mult)\
                    .then_inc(products_ready, 1)

            def mask_decay(k):
                kk = k - 1
                if kk.inside(0, TILES):
                    pool.wait_ge(logs_spread[kk.const % TILE_RING][0], spread_count(kk))
                    pool.wait_ge(logs_spread[kk.const % TILE_RING][1], spread_count(kk))
                pool.wait_ge(maskf_ready, k.times(1, 1))
                pool.sem_inc(held_gpsimd, 1)
                nc.gpsimd.tensor_scalar(logs_n[:, :, 0:J], maskf[:, :].rearrange("p (t j) -> p t j", t=BLOCKS),
                                        -MASKED, MASKED, ALU.mult, ALU.add)\
                    .then_inc(penalty_ready, 1)
                pool.wait_ge(age_exp_ready, k.times(1, 1))
                nc.gpsimd.tensor_tensor(decay[:, :], decay[:, :], maskf[:, :], ALU.mult).then_inc(decay_ready, 1)

            def sum_logs(k):
                pool.wait_ge(log_ready, k.times(1, 1))
                pool.wait_ge(penalty_ready, k.times(1, 1))
                nc.gpsimd.tensor_tensor(logs_n[:, :, 0:J], decay[:, :].rearrange("p (t j) -> p t j", t=BLOCKS),
                                        logs_n[:, :, 0:J], ALU.add)\
                    .then_inc(logs_summed, 1)

            def fetch_windows(k, first, end):
                if first == 0:
                    pool.wait_ge(row_idx_ready, k.times(1, 1))
                    if k.due(WINDOW + 1, -1):
                        pool.wait_ge(short_sums, k.times(WINDOW + 1, -1))
                    pool.sem_inc(held_gpsimd, 1)
                for w in range(first, end):
                    nc.gpsimd.indirect_dma_start(
                        out=window[:, w, :], out_offset=None, in_=rows[:, :],
                        in_offset=bass.IndirectOffsetOnAxis(ap=row_idx[k.const % TILE_RING][:, 0:1], axis=0),
                        element_offset=w * D).then_inc(window_loaded, 16)

            def step(i):
                even, odd = i.const % 2 == 0, i.const % 2 == 1
                fetch, kf = even and i.inside(4, GROUPS), (i - 4).per(2)
                if even and i.inside(-2, GROUPS - 2):
                    sum_logs((i + 2).per(2))
                if (i - 1).inside(0, GROUPS):
                    multiply(i - 1, 2)
                if fetch:
                    fetch_windows(kf, 3, 4)
                if (i - 1).inside(0, GROUPS):
                    multiply(i - 1, 3)
                if fetch:
                    fetch_windows(kf, 4, WINDOW)
                if i.inside(0, GROUPS):
                    multiply(i, 0)
                if odd and i.inside(-3, GROUPS - 3):
                    mask_decay((i + 3).per(2))
                if i.inside(0, GROUPS):
                    multiply(i, 1)
                if odd and i.inside(3, GROUPS):
                    fetch_windows((i - 3).per(2), 0, 3 if (i + 1).inside(0, GROUPS) else 2)
                if even and i.inside(4, GROUPS + 4) and not i.inside(4, GROUPS):
                    fetch_windows(kf, 2 if (i - 1).inside(0, GROUPS) else 0, WINDOW)

            run_steps(pool, step, -3, GROUPS + 2)

        @block.scalar
        def _(act):
            nc.scalar.preload_act_table_set("natural_log_exp_and_others")
            act.dma_start(alpha[:, 0:1], decay_alpha.to_broadcast([P, 1])).then_inc(alpha_loaded, 16)
            act.dma_start(wq_sb, Wq).then_inc(weights_loaded, 16)
            act.dma_start(wk_sb, Wk).then_inc(weights_loaded, 16)
            act.dma_start(wv_sb, Wv).then_inc(weights_loaded, 16)
            act.dma_start(gw[:, :], gate_w.to_broadcast([P, 2])).then_inc(consts_loaded, 16)
            act.dma_start(gb[:, :], gate_b.to_broadcast([P, 1])).then_inc(consts_loaded, 16)
            act.dma_start(gamma[:, :], ln_gamma.to_broadcast([P, D])).then_inc(consts_loaded, 16)
            act.dma_start(beta[:, :], ln_beta.to_broadcast([P, D])).then_inc(consts_loaded, 16)
            act.wait_ge(alpha_v, 2)
            nc.scalar.activation(alpha[:, 3:4], alpha[:, 2:3], ACT.Exp, scale=-1.0).then_inc(alpha_a, 1)
            act.wait_ge(alpha_a, 1)
            nc.scalar.activation(alpha[:, 4:5], alpha[:, 3:4], ACT.Ln, bias=1.0).then_inc(alpha_a, 1)
            act.wait_ge(alpha_v, 5)
            act.wait_ge(consts_built, 8)

            def exp_age(k):
                act.wait_ge(users_loaded, k.times(48, 48))
                if k.due(1):
                    act.wait_ge(logs_summed, k.times(1))
                nc.scalar.activation(decay[:, :], age_n[:, :], ACT.Exp, scale=alpha[:, 7:8]).then_inc(age_exp_ready, 1)

            def log_decay(k):
                act.wait_ge(decay_ready, k.times(1, 1))
                nc.scalar.activation(decay[:, :], decay[:, :], ACT.Ln, bias=tiny[:, 0:1]).then_inc(log_ready, 1)

            def exp_gate(k):
                act.wait_ge(gate_chain, k.times(5, 5))
                nc.scalar.activation(ez, abs_z, ACT.Exp, scale=-1.0).then_inc(gate_exp, 1)

            def sum_products(g, c, first, end):
                if first == 0:
                    act.wait_ge(products_ready, g.times(CHUNKS, c + 1))
                for j in range(first, end):
                    ins = nc.scalar.activation(products[c % 2][:, j, :], products[c % 2][:, j, :], ACT.Copy,
                                               accum_out=raw[g.const % 2][:, c, SV + j:SV + j + 1])
                if end == SP_:
                    ins.then_inc(scored_a, 1)

            def exponentials(g):
                act.wait_ge(shifted, g.times(1, 1))
                if g.due(1):
                    act.wait_ge(exp_sums_ready, g.times(1))
                if g.due(2):
                    act.wait_ge(attn_w_ready, g.times(2))
                nc.scalar.activation(exps[:, :, :], logits[:, :, :], ACT.Exp).then_inc(exps_ready, 1)

            def copy_attended(g):
                act.wait_ge(inv_den_ready, g.times(1, 1))
                if g.due(1):
                    act.wait_ge(attended_turned, g.times(1))
                for h in range(2):
                    ins = nc.scalar.activation(attended[:, h, :], attn_ps[:, (D + 1) * h:(D + 1) * h + D], ACT.Copy,
                                               scale=inv_den[:, h:h + 1])
                ins.then_inc(attended_ready, 1)

            def copy_attended_t(k):
                act.wait_ge(attended_turned, k.times(2, 2))
                if k.due(1):
                    act.wait_ge(long_ready, k.times(1))
                nc.scalar.activation(attended_t[:, :], attended_t_ps, ACT.Copy).then_inc(attended_copied, 1)

            def copy_sums(g, h):
                act.wait_ge(sums_ready, g.times(2, h + 1))
                if g.due(2, h):
                    act.wait_ge(mean_turned, g.times(2, h))
                nc.scalar.activation(sums_sb[:, :], sums_ps[h][:, 0:D], ACT.Copy).then_inc(sums_copied, 1)

            def copy_mean(g, h):
                act.wait_ge(mean_turned, g.times(2, h + 1))
                if g.due(2, h):
                    act.wait_ge(query_ready, g.times(2, h))
                nc.scalar.activation(mean_t[:, :, :], mean_t_ps.rearrange("p (b t) -> p b t", t=1)
                                     .to_broadcast([P, PAIR * USERS_PER_CHUNK, BLOCKS]), ACT.Copy)\
                    .then_inc(mean_copied, 1)

            def copy_query(g, h):
                if g.due(CHUNKS, PAIR * (h + 1) - CHUNKS):
                    act.wait_ge(products_ready, g.times(CHUNKS, PAIR * (h + 1) - CHUNKS))
                act.wait_ge(query_ready, g.times(2, h + 1))
                nc.scalar.activation(query_sb[h][:, :, :].rearrange("p c d -> p (c d)"), query_ps[h][:, 0:PAIR * D],
                                     ACT.Copy).then_inc(query_copied, 1)

            def inverse_deviation(k):
                act.wait_ge(stats_ready, k.times(2, 2))
                nc.scalar.activation(ln_var, mean_var1, ACT.Ln, bias=tiny[:, 1:2]).then_inc(ln_var_ready, 1)
                act.wait_ge(ln_var_ready, k.times(1, 1))
                nc.scalar.activation(rstd, ln_var, ACT.Exp, scale=-0.5).then_inc(rstd_ready, 1)

            def store(k):
                act.wait_ge(result_ready, k.times(1, 1))
                act.dma_start(out_t[k.times(1)], result[:, :]).then_inc(stored, 16)

            def step(i):
                even, odd = i.const % 2 == 0, i.const % 2 == 1
                load, behind = i.inside(0, GROUPS), (i - 1).inside(0, GROUPS)
                gates, kg = odd and i.inside(-1, GROUPS - 1), (i + 1).per(2)
                prepare, kp = odd and i.inside(-3, GROUPS - 3), (i + 3).per(2)
                finish, kf = odd and i.inside(5, GROUPS + 5), (i - 5).per(2)
                if even and i.inside(6, GROUPS + 6):
                    store((i - 6).per(2))
                if load:
                    copy_sums(i, 0)
                if behind:
                    sum_products(i - 1, 2, 0, 6)
                if load:
                    copy_mean(i, 0)
                if behind:
                    sum_products(i - 1, 2, 6, SP_)
                if load:
                    copy_query(i, 0)
                if even and i.inside(4, GROUPS):
                    copy_attended_t((i - 4).per(2))
                if behind:
                    sum_products(i - 1, 3, 0, SP_)
                if even and i.inside(4, GROUPS + 4) and not i.inside(4, GROUPS):
                    copy_attended_t((i - 4).per(2))
                if gates:
                    exp_gate(kg)
                if finish:
                    inverse_deviation(kf)
                if prepare:
                    exp_age(kp)
                if load:
                    copy_sums(i, 1)
                    sum_products(i, 0, 0, 6)
                    copy_mean(i, 1)
                    sum_products(i, 0, 6, SP_)
                if prepare:
                    log_decay(kp)
                last = load and not (i + 1).inside(0, GROUPS)
                if last:
                    copy_query(i, 1)
                if load:
                    sum_products(i, 1, 0, 2)
                if behind:
                    exponentials(i - 1)
                if load and not last:
                    copy_query(i, 1)
                if load:
                    sum_products(i, 1, 2, SP_)
                if (i - 2).inside(0, GROUPS):
                    copy_attended(i - 2)

            run_steps(act, step, -3, GROUPS + 4)
            act.wait_ge(stored, 16 * TILES)

        @block.tensor
        def _(pe):
            pe.wait_ge(weights_loaded, 16 * 3)
            pe.wait_ge(consts_built, 13)
            pe.matmul(max_ps[:, 0:D], wq_sb, wk_sb, start=True, stop=True).then_inc(weights_ps, 1)
            pe.transpose(val_ps[:, 0:D], wv_sb, ident[:, :]).then_inc(weights_ps, 1)
            pe.wait_ge(weights_ready, 2)
            pe.wait_ge(psum_cleared, 4)

            def masked_sums(g, h, q):
                if q == 0:
                    pe.wait_ge(mask_w_ready, g.times(1, 1))
                    if g.due(2, h - 1):
                        pe.wait_ge(sums_copied, g.times(2, h - 1))
                pe.wait_ge(x_loaded[g.const % X_SLOTS][HALVES * h + q], g.per(X_SLOTS).times(16, 16))
                first, end = HALF[q], HALF[q + 1]
                for j in range(first, end):
                    for c in range(PAIR):
                        at = STRIP * (2 * c + j % 2)
                        mm = pe.matmul(sums_ps[h][at:at + USERS_PER_CHUNK, 0:D],
                                       mask_w[g.const % 2][:, PAIR * h + c, j, :],
                                       x[g.const % X_SLOTS][:, PAIR * h + c, j, :], start=(j < 2), stop=(j >= J - 2))
                if q == HALVES - 1:
                    mm.then_inc(sums_ready, 1)

            def turn_sums(g, h):
                pe.wait_ge(sums_copied, g.times(2, h + 1))
                pe.matmul(mean_t_ps, sums_sb[:, :], pick[:, :, :].rearrange("p c b -> p (c b)"),
                          start=True, stop=True).then_inc(mean_turned, 1)

            def queries(g, h):
                pe.wait_ge(mean_copied, g.times(2, h + 1))
                if g.due(2 * CHUNKS, 2 * (PAIR * (h + 1) - CHUNKS)):
                    pe.wait_ge(scored_v, g.times(2 * CHUNKS, 2 * (PAIR * (h + 1) - CHUNKS)))
                for c in range(PAIR):
                    users = mean_t[:, USERS_PER_CHUNK * c:USERS_PER_CHUNK * (c + 1), :]
                    mm = pe.matmul(query_ps[h][:, D * c:D * (c + 1)], users.rearrange("p b t -> p (b t)"),
                                   qk[:, :], start=True, stop=True)
                mm.then_inc(query_ready, 1)

            def turn_maxes(g):
                pe.wait_ge(maxes_ready, g.times(1, 1))
                pe.transpose(max_t_ps, maxes[:, :], ident[:, :]).then_inc(maxes_turned, 1)

            def spread_gmax(g):
                pe.wait_ge(gmax_ready, g.times(2, 2))
                pe.matmul(max_p_ps, gmax_wide[:, :, :].rearrange("c b t -> c (b t)"),
                          ident[0:CHUNKS, 0:CHUNKS], start=True, stop=True).then_inc(gmax_spread, 1)

            def attention_sums(g, h, first, end):
                if first == 0:
                    pe.wait_ge(attn_w_ready, g.times(2, h + 1))
                if h == 0 and first == 0:
                    if g.due(1):
                        pe.wait_ge(attended_ready, g.times(1))
                at_h = (D + 1) * h
                for j in range(first, end):
                    for c in range(PAIR):
                        at = STRIP * (2 * c + j % 2)
                        mm = pe.matmul(attn_ps[at:at + USERS_PER_CHUNK, at_h:at_h + D],
                                       attn_w[:, PAIR * h + c, j, :], x[g.const % X_SLOTS][:, PAIR * h + c, j, :],
                                       start=(j < 2), stop=(j >= J - 2))
                if end == J:
                    mm.then_inc(x_free, 1)

            def softmax_denominators(g):
                pe.wait_ge(exp_sums_ready, g.times(1, 1))
                for h in range(2):
                    for c in range(PAIR):
                        for at in (2 * STRIP * c, 2 * STRIP * c + STRIP):
                            mm = pe.matmul(attn_ps[at:at + USERS_PER_CHUNK, (D + 1) * h + D:(D + 1) * (h + 1)],
                                           own[:, :], exp_sums[:, PAIR * h + c:PAIR * h + c + 1],
                                           start=True, stop=True)
                mm.then_inc(attn_sums_ready, 1)

            def turn_attended(g):
                pe.wait_ge(attended_ready, g.times(1, 1))
                if g.per(2).due(1):
                    pe.wait_ge(attended_copied, g.per(2).times(1))
                for h in range(2):
                    at = GROUP * (g.const % 2) + PAIR * USERS_PER_CHUNK * h
                    mm = pe.matmul(attended_t_ps[:, at:at + PAIR * USERS_PER_CHUNK], attended[:, h, :],
                                   pick[:, :, :].rearrange("p c b -> p (c b)"), start=True, stop=True)
                mm.then_inc(attended_turned, 1)

            def project_values(k):
                pe.wait_ge(attended_copied, k.times(1, 1))
                pe.wait_ge(shifted, k.times(2, 4 if (k + 1).inside(0, TILES) else 2))
                pe.matmul(long_ps, attended_t[:, :], wv_t[:, :], start=True, stop=True).then_inc(long_ready, 1)

            def step(i):
                load, attend, g = i.inside(0, GROUPS), (i - 2).inside(0, GROUPS), i - 2
                if i.const % 2 == 1 and i.inside(5, GROUPS + 5):
                    project_values((i - 5).per(2))
                if load:
                    masked_sums(i, 0, 0)
                    masked_sums(i, 0, 1)
                if attend:
                    attention_sums(g, 0, 0, 8)
                if load:
                    turn_sums(i, 0)
                if attend:
                    attention_sums(g, 0, 8, J)
                if load:
                    queries(i, 0)
                if (i - 3).inside(0, GROUPS):
                    turn_attended(i - 3)
                if load:
                    masked_sums(i, 1, 0)
                    masked_sums(i, 1, 1)
                if attend:
                    attention_sums(g, 1, 0, 8)
                if load:
                    turn_sums(i, 1)
                if attend:
                    attention_sums(g, 1, 8, 16)
                if (i - 1).inside(0, GROUPS):
                    turn_maxes(i - 1)
                last = load and not (i + 1).inside(0, GROUPS)
                if last:
                    queries(i, 1)
                if attend:
                    attention_sums(g, 1, 16, J)
                    softmax_denominators(g)
                if (i - 1).inside(0, GROUPS):
                    spread_gmax(i - 1)
                if load and not last:
                    queries(i, 1)

            run_steps(pe, step, 0, GROUPS + 3)

        @block.vector
        def _(dve):
            for bank in (sums_ps[0], sums_ps[1], attn_ps):
                nc.vector.memset(bank[:, :], 0.0).then_inc(psum_cleared, 1)
            dve.wait_ge(psum_cleared, 3)
            nc.vector.memset(dens_ps, 1.0).then_inc(psum_cleared, 1)
            dve.wait_ge(consts_built, 8)
            nc.vector.tensor_copy(times[:, :], times_i).then_inc(consts_cast, 1)
            nc.vector.tensor_copy(row_base[:, :], base_i[:, :]).then_inc(consts_cast, 1)
            dve.wait_ge(alpha_loaded, 16)
            nc.vector.tensor_scalar(alpha[:, 1:2], alpha[:, 0:1], -1.0, None, ALU.mult).then_inc(alpha_v, 1)
            dve.wait_ge(alpha_v, 1)
            nc.vector.tensor_tensor(alpha[:, 2:3], alpha[:, 0:1], alpha[:, 1:2], ALU.max).then_inc(alpha_v, 1)
            nc.vector.tensor_scalar(alpha[:, 5:6], alpha[:, 0:1], 0.0, None, ALU.max).then_inc(alpha_v, 1)
            dve.wait_ge(alpha_v, 3)
            dve.wait_ge(alpha_a, 2)
            nc.vector.tensor_tensor(alpha[:, 6:7], alpha[:, 5:6], alpha[:, 4:5], ALU.add).then_inc(alpha_v, 1)
            dve.wait_ge(alpha_v, 4)
            nc.vector.tensor_scalar(alpha[:, 7:8], alpha[:, 6:7], 1e-6, -1.0, ALU.add, ALU.mult).then_inc(alpha_v, 1)
            dve.wait_ge(consts_cast, 2)

            def build_mask_weights(g):
                k = g.per(2)
                dve.wait_ge(logs_spread[k.const % TILE_RING][g.const % 2], spread_count(k))
                if g.due(2, -2):
                    dve.wait_ge(sums_ready, g.times(2, -2))
                logs = logs_p[g.const % UNROLL]
                for c in range(CHUNKS):
                    w = nc.vector.scalar_tensor_tensor(
                        out=mask_w[g.const % 2][:, c, :, :],
                        in0=logs[:, c, 0:J].rearrange("p (j b) -> p j b", b=1).to_broadcast([P, J, USERS_PER_CHUNK]),
                        scalar=MASKED / 2,
                        in1=own[:, :].rearrange("p (j b) -> p j b", j=1).to_broadcast([P, J, USERS_PER_CHUNK]),
                        op0=ALU.is_gt, op1=ALU.mult)
                w.then_inc(mask_w_ready, 1)

            def score(g, c, first, end):
                h = c // PAIR
                if first == 0 and c % PAIR == 0:
                    dve.wait_ge(query_copied, g.times(2, h + 1))
                for j in range(first, end):
                    if j in (0, SV_HALF):
                        if g.due(2 * CHUNKS, 2 * c - 1 + (j > 0)):
                            dve.wait_ge(scored_v, g.times(2 * CHUNKS, 2 * c - 1 + (j > 0)))
                    ins = nc.vector.tensor_tensor_reduce(
                        unused_v[:, j, :], x[g.const % X_SLOTS][:, c, j, :],
                        query_ps[h][:, D * (c % PAIR):D * (c % PAIR + 1)],
                        1.0, 0.0, ALU.mult, ALU.add, raw[g.const % 2][:, c, j:j + 1])
                    if j in (SV_HALF - 1, SV - 1):
                        ins.then_inc(scored_v, 1)

            def scale_logits(g):
                dve.wait_ge(scored_a, g.times(CHUNKS, CHUNKS))
                dve.wait_ge(scored_v, g.times(2 * CHUNKS, 2 * CHUNKS))
                if g.due(1):
                    dve.wait_ge(exps_ready, g.times(1))
                logs = logs_p[g.const % UNROLL]
                nc.vector.tensor_tensor(logits[:, :, :], raw[g.const % 2][:, :, :],
                                        logs[:, :, J:J + 1].to_broadcast([P, CHUNKS, J]), ALU.mult)\
                    .then_inc(logits_scaled, 1)

            def add_logs(g):
                dve.wait_ge(logits_scaled, g.times(1, 1))
                nc.vector.tensor_tensor(logits[:, :, :], logits[:, :, :], logs_p[g.const % UNROLL][:, :, 0:J], ALU.add)\
                    .then_inc(logits_ready, 1)

            def partition_maxes(g):
                dve.wait_ge(logits_ready, g.times(1, 1))
                nc.vector.tensor_reduce(maxes[:, :], logits[:, :, :], AX_X, ALU.max).then_inc(maxes_ready, 1)

            def user_maxes(g):
                dve.wait_ge(maxes_turned, g.times(1, 1))
                nc.vector.tensor_reduce(gmax[:, :], max_t_ps.rearrange("c (b t) -> c b t", t=BLOCKS), AX_X, ALU.max)\
                    .then_inc(gmax_ready, 1)

            def widen_maxes(g):
                dve.wait_ge(gmax_ready, g.times(2, 1))
                nc.vector.tensor_copy(gmax_wide[:, :, :], gmax[:, :].rearrange("c (b t) -> c b t", t=1)
                                      .to_broadcast([CHUNKS, USERS_PER_CHUNK, BLOCKS])).then_inc(gmax_ready, 1)

            def shift(g):
                dve.wait_ge(gmax_spread, g.times(1, 1))
                nc.vector.tensor_tensor(logits[:, :, :], logits[:, :, :],
                                        max_p_ps.rearrange("p (c j) -> p c j", j=1).to_broadcast([P, CHUNKS, J]),
                                        ALU.subtract).then_inc(shifted, 1)

            def build_attention_weights(g):
                dve.wait_ge(exps_ready, g.times(1, 1))
                for h in range(2):
                    if g.due(2, h - 1):
                        dve.wait_ge(x_free, g.times(2, h - 1))
                    nc.vector.tensor_tensor(
                        attn_w[:, PAIR * h:PAIR * (h + 1), :, :].rearrange("p c j b -> p (c j) b"),
                        exps[:, PAIR * h:PAIR * (h + 1), :].rearrange("p c (j b) -> p (c j) b", b=1)
                        .to_broadcast([P, PAIR * J, USERS_PER_CHUNK]),
                        own[:, :].rearrange("p (j b) -> p j b", j=1).to_broadcast([P, PAIR * J, USERS_PER_CHUNK]),
                        ALU.mult).then_inc(attn_w_ready, 1)
                if g.due(1):
                    dve.wait_ge(attn_sums_ready, g.times(1))
                nc.vector.tensor_reduce(exp_sums[:, :], exps[:, :, :], AX_X, ALU.add).then_inc(exp_sums_ready, 1)

            def invert_denominators(g):
                dve.wait_ge(attn_sums_ready, g.times(1, 1))
                if g.due(1):
                    dve.wait_ge(attended_ready, g.times(1))
                nc.vector.reciprocal(inv_den[:, :], dens_ps).then_inc(inv_den_ready, 1)

            def copy_weights():
                dve.wait_ge(weights_ps, 2)
                nc.vector.tensor_copy(qk[:, :], max_ps[:, 0:D]).then_inc(weights_ready, 1)
                nc.vector.tensor_copy(wv_t[:, :], val_ps[:, 0:D]).then_inc(weights_ready, 1)

            def count_masks(k):
                dve.wait_ge(users_loaded, k.times(48, 48))
                if k.due(1):
                    dve.wait_ge(decay_ready, k.times(1))
                if k.due(1):
                    dve.wait_ge(penalty_ready, k.times(1))
                nc.vector.tensor_scalar(maskf[:, :], mask_n[:, :], 1.0, None, ALU.mult, ALU.add, accum_out=cnt)\
                    .then_inc(maskf_ready, 1)

            def start_scale(k):
                dve.wait_ge(maskf_ready, k.times(1, 1))
                nc.vector.tensor_scalar(cnt_eps, cnt, 1e-6, None, ALU.add).then_inc(scale_chain, 1)

            def invert_scale(k):
                dve.wait_ge(scale_chain, k.times(2, 1))
                nc.vector.reciprocal(inv_eps, cnt_eps).then_inc(scale_chain, 1)

            def place_scale(k):
                dve.wait_ge(scale_chain, k.times(2, 2))
                kk = k - 1
                if kk.inside(0, TILES):
                    dve.wait_ge(logs_spread[kk.const % TILE_RING][0], spread_count(kk))
                    dve.wait_ge(logs_spread[kk.const % TILE_RING][1], spread_count(kk))
                nc.vector.tensor_scalar(logs_n[:, :, J], ones8[:, :], inv_eps, SCALE, ALU.mult, ALU.mult)\
                    .then_inc(scale_ready, 1)

            def bound_counts(k):
                dve.wait_ge(maskf_ready, k.times(1, 1))
                nc.vector.tensor_scalar(cnt1, cnt, 1.0, None, ALU.max).then_inc(user_counts, 1)
                nc.vector.tensor_scalar(cnt_min, cnt, 1.0, None, ALU.min).then_inc(user_counts, 1)

            def invert_counts(k):
                dve.wait_ge(user_counts, k.times(2, 2))
                nc.vector.tensor_scalar(denom, cnt1, float(WINDOW), None, ALU.min).then_inc(user_derived, 1)
                nc.vector.reciprocal(inv_min, cnt_min).then_inc(user_derived, 1)
                nc.vector.tensor_scalar(below[:, :], times[:, :], cnt1, None, ALU.is_lt).then_inc(user_windows, 1)

            def place_windows(k):
                dve.wait_ge(user_derived, k.times(2, 2))
                nc.vector.tensor_tensor(start, cnt1, denom, ALU.subtract).then_inc(user_windows, 1)
                nc.vector.reciprocal(inv_denom, denom).then_inc(user_windows, 1)

            def window_weights(k):
                dve.wait_ge(user_windows, k.times(4, 3))
                if k.due(1):
                    dve.wait_ge(row_base_moved, k.times(1))
                if k.due(16 * WINDOW, 16 * WINDOW * (1 - TILE_RING)):
                    dve.wait_ge(window_loaded, k.times(16 * WINDOW, 16 * WINDOW * (1 - TILE_RING)))
                nc.vector.tensor_tensor(row_idx[k.const % TILE_RING][:, :], start, row_base[:, :], ALU.add)\
                    .then_inc(row_idx_ready, 1)
                nc.vector.tensor_scalar(win_w[:, :], times[:, 0:WINDOW], denom, inv_denom, ALU.is_lt, ALU.mult)\
                    .then_inc(user_windows, 1)
                nc.vector.scalar_tensor_tensor(out=below[:, :], in0=times[:, :], scalar=start, in1=below[:, :],
                                               op0=ALU.is_ge, op1=ALU.mult).then_inc(lastk_ready, 1)

            def window_sums(k):
                dve.wait_ge(row_idx_ready, k.times(1, 1))
                nc.vector.tensor_scalar(row_base[:, :], row_base[:, :], float(P * T), None, ALU.add)\
                    .then_inc(row_base_moved, 1)
                dve.wait_ge(lastk_ready, k.times(1, 1))
                nc.vector.tensor_tensor_reduce(pop_n[:, :], pop_n[:, :], below[:, :], 1.0, 0.0, ALU.mult, ALU.add,
                                               pop_sum).then_inc(ctx_sums, 1)
                dve.wait_ge(age_exp_ready, k.times(1, 1))
                nc.vector.tensor_tensor_reduce(age_n[:, :], age_n[:, :], below[:, :], 1.0, 0.0, ALU.mult, ALU.add,
                                               age_sum).then_inc(ctx_sums, 1)

            def gate_logit_pop(k):
                dve.wait_ge(ctx_sums, k.times(2, 2))
                nc.vector.tensor_scalar(z1, pop_sum, gw[:, 0:1], None, ALU.mult).then_inc(gate_chain, 1)

            def gate_logit_age(k):
                dve.wait_ge(gate_chain, k.times(5, 1))
                nc.vector.scalar_tensor_tensor(out=z2, in0=age_sum, scalar=gw[:, 1:2], in1=z1, op0=ALU.mult,
                                               op1=ALU.add).then_inc(gate_chain, 1)

            def gate_logit(k):
                dve.wait_ge(gate_chain, k.times(5, 2))
                nc.vector.tensor_scalar(z, z2, inv_denom, gb[:, 0:1], ALU.mult, ALU.add).then_inc(gate_chain, 1)

            def gate_magnitude(k):
                dve.wait_ge(gate_chain, k.times(5, 3))
                nc.vector.scalar_tensor_tensor(out=abs_z, in0=z, scalar=-1.0, in1=z, op0=ALU.mult, op1=ALU.max)\
                    .then_inc(gate_chain, 1)
                nc.vector.tensor_scalar(positive, z, 0.0, None, ALU.is_ge).then_inc(gate_chain, 1)

            def gate_denominator(k):
                dve.wait_ge(gate_exp, k.times(1, 1))
                nc.vector.tensor_scalar(e1, ez, 1.0, None, ALU.add).then_inc(gate_tail, 1)

            def gate_large(k):
                dve.wait_ge(gate_tail, k.times(6, 1))
                nc.vector.reciprocal(large, e1).then_inc(gate_tail, 1)

            def gate_small(k):
                dve.wait_ge(gate_tail, k.times(6, 2))
                nc.vector.tensor_tensor(small, ez, large, ALU.mult).then_inc(gate_tail, 1)

            def gate_gap(k):
                dve.wait_ge(gate_tail, k.times(6, 3))
                nc.vector.tensor_tensor(gap, large, small, ALU.subtract).then_inc(gate_tail, 1)

            def gate_value(k):
                dve.wait_ge(gate_tail, k.times(6, 4))
                nc.vector.scalar_tensor_tensor(out=gate, in0=gap, scalar=positive, in1=small, op0=ALU.mult,
                                               op1=ALU.add).then_inc(gate_tail, 1)

            def gate_rest(k):
                dve.wait_ge(gate_tail, k.times(6, 5))
                nc.vector.tensor_scalar(omg, gate, -1.0, 1.0, ALU.mult, ALU.add).then_inc(gate_tail, 1)

            def gate_weights(k):
                dve.wait_ge(user_windows, k.times(4, 4))
                nc.vector.tensor_scalar(gate_win[k.const % TILE_RING][:, :], win_w[:, :], gate, None, ALU.mult)\
                    .then_inc(gates_ready, 1)
                dve.wait_ge(gate_tail, k.times(6, 6))
                nc.vector.tensor_tensor(gate_long[k.const % TILE_RING][:, :], omg, inv_min, ALU.mult)\
                    .then_inc(gates_ready, 1)

            def short_term(k, w):
                if w == 0:
                    dve.wait_ge(window_loaded, k.times(16 * WINDOW, 16 * WINDOW))
                    dve.wait_ge(gates_ready, k.times(2, 2))
                    nc.vector.tensor_scalar(user[:, :], window[:, 0, :], gate_win[k.const % TILE_RING][:, 0:1], None,
                                            ALU.mult).then_inc(short_sums, 1)
                else:
                    dve.wait_ge(short_sums, k.times(WINDOW + 1, w))
                    nc.vector.scalar_tensor_tensor(out=user[:, :], in0=window[:, w, :],
                                                   scalar=gate_win[k.const % TILE_RING][:, w:w + 1], in1=user[:, :],
                                                   op0=ALU.mult, op1=ALU.add).then_inc(short_sums, 1)

            def add_long_term(k):
                dve.wait_ge(long_ready, k.times(1, 1))
                dve.wait_ge(short_sums, k.times(WINDOW + 1, WINDOW))
                nc.vector.scalar_tensor_tensor(out=user[:, :], in0=long_ps, scalar=gate_long[k.const % TILE_RING][:, 0:1],
                                               in1=user[:, :], op0=ALU.mult, op1=ALU.add).then_inc(short_sums, 1)

            def measure(k):
                dve.wait_ge(short_sums, k.times(WINDOW + 1, WINDOW + 1))
                nc.vector.bn_stats(stats[:, :], user[:, :]).then_inc(stats_ready, 1)

            def measure_all(k):
                dve.wait_ge(stats_ready, k.times(2, 1))
                dve.sem_inc(held_vector, 1)
                nc.vector.bn_aggr(mean_var, stats[:, :]).then_inc(stats_ready, 1)

            def centre(k):
                dve.wait_ge(stats_ready, k.times(2, 2))
                if k.due(16):
                    dve.wait_ge(stored, k.times(16))
                nc.vector.scalar_tensor_tensor(out=result[:, :], in0=user[:, :], scalar=mean_var0, in1=gamma[:, :],
                                               op0=ALU.subtract, op1=ALU.mult).then_inc(centred, 1)

            def normalise(k):
                dve.wait_ge(rstd_ready, k.times(1, 1))
                dve.wait_ge(centred, k.times(1, 1))
                nc.vector.scalar_tensor_tensor(out=result[:, :], in0=result[:, :], scalar=rstd, in1=beta[:, :],
                                               op0=ALU.mult, op1=ALU.add).then_inc(result_ready, 1)

            def step(i):
                g, d, odd = i - 1, i - 1, i.const % 2 == 1
                behind, ahead = g.inside(0, GROUPS), i.inside(0, GROUPS)
                logs, kl = not odd and i.inside(-2, GROUPS - 2), (i + 2).per(2)
                prepare, kp = odd and i.inside(-3, GROUPS - 3), (i + 3).per(2)
                gates, kg = odd and i.inside(-1, GROUPS - 1), (i + 1).per(2)
                finish, kf = odd and i.inside(5, GROUPS + 5), (i - 5).per(2)

                short, ks = i.const % 2 == 0 and i.inside(4, GROUPS + 4), (i - 4).per(2)

                def part(c, first, end):
                    if c >= PAIR and behind:
                        score(g, c, first, end)
                    if c < PAIR and ahead:
                        score(i, c, first, end)

                part(2, 0, 2)
                if logs:
                    bound_counts(kl)
                if gates:
                    window_weights(kg)
                part(2, 2, 5)
                if gates:
                    window_sums(kg)
                if logs:
                    invert_counts(kl)
                part(2, 5, 8)
                if logs:
                    place_windows(kl)
                part(2, 8, 11)
                part(2, 11, SV)
                part(3, 0, 2)
                part(3, 2, 5)
                if i.it is None and i.const == -1:
                    copy_weights()
                    dve.wait_ge(consts_loaded, 16 * 4)
                if gates:
                    gate_logit_pop(kg)
                part(3, 5, 8)
                if gates:
                    gate_logit_age(kg)
                if finish:
                    add_long_term(kf)
                part(3, 8, 11)
                if gates:
                    gate_logit(kg)
                if finish:
                    measure(kf)
                part(3, 11, SV)
                if gates:
                    gate_magnitude(kg)
                if finish:
                    measure_all(kf)
                if prepare and ahead:
                    count_masks(kp)
                part(0, 0, 2)
                if not (odd and ahead) and (i + 1).inside(0, GROUPS):
                    build_mask_weights(i + 1)
                if prepare and not ahead:
                    count_masks(kp)
                if prepare:
                    start_scale(kp)
                part(0, 2, 5)
                if prepare:
                    invert_scale(kp)
                if behind:
                    scale_logits(d)
                part(0, 5, 7)
                if prepare:
                    place_scale(kp)
                if behind:
                    add_logs(d)
                part(0, 7, 9)
                if behind:
                    partition_maxes(d)
                if finish:
                    centre(kf)
                part(0, 9, SV)
                if behind:
                    user_maxes(d)
                if finish:
                    normalise(kf)
                if gates:
                    gate_denominator(kg)
                part(1, 0, 2)
                if behind:
                    widen_maxes(d)
                if short and not ahead:
                    for w in range(WINDOW):
                        short_term(ks, w)
                if odd and ahead and (i + 1).inside(0, GROUPS):
                    build_mask_weights(i + 1)
                if gates:
                    gate_large(kg)
                part(1, 2, 5)
                if behind:
                    shift(d)
                if gates:
                    gate_small(kg)
                part(1, 5, 7)
                if gates:
                    gate_gap(kg)
                part(1, 7, 9)
                if gates:
                    gate_value(kg)
                part(1, 9, 11)
                if gates:
                    gate_rest(kg)
                if (i - 2).inside(0, GROUPS):
                    invert_denominators(i - 2)
                if behind:
                    build_attention_weights(d)
                if gates:
                    gate_weights(kg)
                if short and ahead:
                    short_term(ks, 0)
                part(1, 11, 12)
                if short and ahead:
                    short_term(ks, 1)
                part(1, 12, SV)
                if short and ahead:
                    for w in range(2, WINDOW):
                        short_term(ks, w)

            run_steps(dve, step, -3, GROUPS + 3)


_INS = ["r_hist_items", "r_hist_mask", "r_hist_age_hours", "r_hist_popularity", "L0_rec_Wq", "L0_rec_Wk",
        "L0_rec_Wv", "L0_rec_gate_w", "L0_rec_gate_b", "L0_rec_ln_gamma", "L0_rec_ln_beta", "L0_rec_decay_alpha"]


def kernel(**inputs):
    import numpy as np
    import concourse.bacc as bacc
    from concourse.bass_utils import run_bass_kernel_spmd

    nc = bacc.Bacc("TRN2", target_bir_lowering=False, num_devices=1)
    arrays, args = {}, []
    for name in _INS:
        a = np.ascontiguousarray(inputs[name])
        if a.ndim < 2:
            a = a.reshape(1, -1)
        arrays[f"in_{name}_dram"] = a
        args.append(nc.dram_tensor(f"in_{name}_dram", a.shape, mybir.dt.from_np(a.dtype), kind="ExternalInput").ap())
    users, _, dims = inputs["r_hist_items"].shape
    out = nc.dram_tensor("out_0_dram", (users, dims), F32, kind="ExternalOutput").ap()
    build(nc, *args, out)
    r = run_bass_kernel_spmd(nc, [arrays], core_ids=[0])
    return r.results[0]["out_0_dram"]
```
